# Optimizing a Trainium2 kernel written in Bass

```python
import numpy as np
import jax
import jax.numpy as jnp

def _softmax(x, axis=-1):
    return jax.nn.softmax(x, axis=axis)

def _gelu(x):
    return jax.nn.gelu(x, approximate=True)

def _silu(x):
    return jax.nn.silu(x)

def _sigmoid(x):
    return jax.nn.sigmoid(x)

def _layernorm(x, axis=-1, eps=1e-05):
    m = jnp.mean(x, axis=axis, keepdims=True)
    v = jnp.var(x, axis=axis, keepdims=True)
    return (x - m) / jnp.sqrt(v + eps)

def _scatter_add(tgt, idx, src, axis=0):
    return tgt.at[idx].add(src)

def _segment_sum(src, seg, n):
    return jax.ops.segment_sum(src, seg, n)
kernel_name = 'mk_lm_tower_d1_tok_ids256_r4_93c154'

def setup_inputs(seed: int=0):
    np.random.seed(seed)
    _w = jnp.asarray

    def _rec_inputs():
        import jax
        import jax.numpy as jnp
        _rk = jax.random.key(seed)
        x = jax.random.randint(jax.random.fold_in(_rk, 1), (16, 1024), 0, 64, jnp.int32)
        return x
    x = _rec_inputs()

    def _L0_tok_setup():
        import jax, jax.numpy as jnp
        import numpy as np
        TWO_PI = 2.0 * 3.14159265
        LN_EPS = 1e-05

        def _spectral_features(byte_ids, D):
            signal = byte_ids.astype(jnp.float32) / 127.5 - 1.0
            T = byte_ids.shape[1]
            pos = jnp.arange(T, dtype=jnp.int32)[:, None]
            dim = jnp.arange(D, dtype=jnp.int32)[None, :]
            phase = TWO_PI * (pos * dim % T).astype(jnp.float32) / T
            cos_p, sin_p = (jnp.cos(phase), jnp.sin(phase))
            s = signal[:, :, None]
            return jnp.sqrt((s * cos_p) ** 2 + (s * sin_p) ** 2)

        def _mlp(feats, W1, b1, ln_g, ln_b, W2, b2):
            h = feats @ W1 + b1
            mu = jnp.mean(h, axis=-1, keepdims=True)
            var = jnp.mean((h - mu) ** 2, axis=-1, keepdims=True)
            h = (h - mu) * jax.lax.rsqrt(var + LN_EPS) * ln_g + ln_b
            h = jax.nn.gelu(h, approximate=False)
            return h @ W2 + b2
        key = jax.random.key(seed)
        k1, k2, k3 = jax.random.split(key, 3)
        B, T, D = (16, 1024, 64)
        byte_ids = jax.random.randint(k1, (B, T), 0, 64, dtype=jnp.int64)
        W1 = jax.random.normal(k2, (D, 2 * D), dtype=jnp.float32) * (1.0 / np.sqrt(D))
        b1 = jnp.zeros((2 * D,), dtype=jnp.float32)
        ln_g = jnp.ones((2 * D,), dtype=jnp.float32)
        ln_b = jnp.zeros((2 * D,), dtype=jnp.float32)
        W2 = jax.random.normal(k3, (2 * D, D), dtype=jnp.float32) * (1.0 / np.sqrt(2 * D))
        b2 = jnp.zeros((D,), dtype=jnp.float32)
        return {'byte_ids': byte_ids, 'W1': W1, 'b1': b1, 'ln_g': ln_g, 'ln_b': ln_b, 'W2': W2, 'b2': b2}
    _L0_tok_all = _L0_tok_setup()
    _L0_tok_in = {k: v for k, v in _L0_tok_all.items() if k in ('W1', 'b1', 'ln_g', 'ln_b', 'W2', 'b2')}
    del _L0_tok_all

    def _L0_attn_setup():
        import jax, jax.numpy as jnp
        import numpy as np
        key = jax.random.key(seed)
        inputs = jax.random.normal(key, (8, 512, 64), dtype=jnp.float32)
        return {'inputs': inputs}
    _L0_attn_all = _L0_attn_setup()
    _L0_attn_in = {k: v for k, v in _L0_attn_all.items() if k in ()}
    del _L0_attn_all

    def _L0_ffn_setup():
        import jax, jax.numpy as jnp
        import numpy as np
        B, T, IN_DIM = (64, 64, 64)
        HID, OUT_DIM = (128, 64)
        N_LAYERS, N_EXPERTS, N_SHARED = (2, 16, 1)
        key = jax.random.key(seed)
        ks = jax.random.split(key, 10)
        s = 0.02
        x = jax.random.normal(ks[0], (B, T, IN_DIM), dtype=jnp.float32)
        route_id = jax.random.randint(ks[1], (B,), 0, N_EXPERTS)
        Wi = jax.random.normal(ks[2], (HID, IN_DIM), dtype=jnp.float32) * s
        bi = jnp.zeros((HID,), dtype=jnp.float32)
        Wr = jax.random.normal(ks[3], (N_LAYERS, N_EXPERTS, HID, HID), dtype=jnp.float32) * s
        br = jax.random.normal(ks[4], (N_LAYERS, N_EXPERTS, HID), dtype=jnp.float32) * s
        Ws = jax.random.normal(ks[5], (N_LAYERS, N_SHARED, HID, HID), dtype=jnp.float32) * s
        bs = jax.random.normal(ks[6], (N_LAYERS, N_SHARED, HID), dtype=jnp.float32) * s
        Wo = jax.random.normal(ks[7], (OUT_DIM, HID), dtype=jnp.float32) * s
        bo = jnp.zeros((OUT_DIM,), dtype=jnp.float32)
        return {'x': x, 'route_id': route_id, 'Wi': Wi, 'bi': bi, 'Wr': Wr, 'br': br, 'Ws': Ws, 'bs': bs, 'Wo': Wo, 'bo': bo}
    _L0_ffn_all = _L0_ffn_setup()
    _L0_ffn_in = {k: v for k, v in _L0_ffn_all.items() if k in ('route_id', 'Wi', 'bi', 'Wr', 'br', 'Ws', 'bs', 'Wo', 'bo')}
    del _L0_ffn_all
    return {'x': x, 'L0_tok_W1': _L0_tok_in['W1'], 'L0_tok_b1': _L0_tok_in['b1'], 'L0_tok_ln_g': _L0_tok_in['ln_g'], 'L0_tok_ln_b': _L0_tok_in['ln_b'], 'L0_tok_W2': _L0_tok_in['W2'], 'L0_tok_b2': _L0_tok_in['b2'], 'L0_ffn_route_id': _L0_ffn_in['route_id'], 'L0_ffn_Wi': _L0_ffn_in['Wi'], 'L0_ffn_bi': _L0_ffn_in['bi'], 'L0_ffn_Wr': _L0_ffn_in['Wr'], 'L0_ffn_br': _L0_ffn_in['br'], 'L0_ffn_Ws': _L0_ffn_in['Ws'], 'L0_ffn_bs': _L0_ffn_in['bs'], 'L0_ffn_Wo': _L0_ffn_in['Wo'], 'L0_ffn_bo': _L0_ffn_in['bo']}

def reference(x, L0_tok_W1, L0_tok_b1, L0_tok_ln_g, L0_tok_ln_b, L0_tok_W2, L0_tok_b2, L0_ffn_route_id, L0_ffn_Wi, L0_ffn_bi, L0_ffn_Wr, L0_ffn_br, L0_ffn_Ws, L0_ffn_bs, L0_ffn_Wo, L0_ffn_bo):
    import jax
    import jax.numpy as jnp

    def _L0_tok_ref(byte_ids, W1, b1, ln_g, ln_b, W2, b2):
        import jax, jax.numpy as jnp
        import numpy as np
        TWO_PI = 2.0 * 3.14159265
        LN_EPS = 1e-05

        def _spectral_features(byte_ids, D):
            signal = byte_ids.astype(jnp.float32) / 127.5 - 1.0
            T = byte_ids.shape[1]
            pos = jnp.arange(T, dtype=jnp.int32)[:, None]
            dim = jnp.arange(D, dtype=jnp.int32)[None, :]
            phase = TWO_PI * (pos * dim % T).astype(jnp.float32) / T
            cos_p, sin_p = (jnp.cos(phase), jnp.sin(phase))
            s = signal[:, :, None]
            return jnp.sqrt((s * cos_p) ** 2 + (s * sin_p) ** 2)

        def _mlp(feats, W1, b1, ln_g, ln_b, W2, b2):
            h = feats @ W1 + b1
            mu = jnp.mean(h, axis=-1, keepdims=True)
            var = jnp.mean((h - mu) ** 2, axis=-1, keepdims=True)
            h = (h - mu) * jax.lax.rsqrt(var + LN_EPS) * ln_g + ln_b
            h = jax.nn.gelu(h, approximate=False)
            return h @ W2 + b2
        feats = _spectral_features(byte_ids, W1.shape[0])
        return _mlp(feats, W1, b1, ln_g, ln_b, W2, b2)

    def _L0_attn_ref(inputs):
        import jax, jax.numpy as jnp
        import numpy as np
        d_k = jnp.asarray(inputs.shape[-1], dtype=inputs.dtype)
        scores = jnp.einsum('bnd,bmd->bnm', inputs, inputs) / jnp.sqrt(d_k)
        weights = jax.nn.softmax(scores, axis=-1)
        context = jnp.einsum('bnm,bmd->bnd', weights, inputs)
        return context

    def _L0_ffn_ref(x, route_id, Wi, bi, Wr, br, Ws, bs, Wo, bo):
        import jax, jax.numpy as jnp
        import numpy as np
        B, T, IN_DIM = (64, 64, 64)
        HID, OUT_DIM = (128, 64)
        N_LAYERS, N_EXPERTS, N_SHARED = (2, 16, 1)
        flat = x.reshape(-1, x.shape[-1])
        n_tok = flat.shape[0]
        route = jnp.repeat(route_id, n_tok // route_id.shape[0])
        h = jax.nn.relu(flat @ Wi.T + bi)
        n_layers, n_experts = (Wr.shape[0], Wr.shape[1])
        for l in range(n_layers):
            shared = (jnp.einsum('nd,shd->snh', h, Ws[l]) + bs[l][:, None, :]).mean(axis=0)
            routed = jnp.zeros_like(h)
            for e in range(n_experts):
                ye = h @ Wr[l, e].T + br[l, e]
                routed = routed + jnp.where((route == e)[:, None], ye, 0.0)
            h = jax.nn.relu(shared + routed + h)
        out = h @ Wo.T + bo
        return out.reshape(*x.shape[:-1], out.shape[-1])
    h = _L0_tok_ref(x, L0_tok_W1, L0_tok_b1, L0_tok_ln_g, L0_tok_ln_b, L0_tok_W2, L0_tok_b2)
    h = h + _L0_attn_ref(_layernorm(h, axis=-1))
    h = h + _L0_ffn_ref(_layernorm(h, axis=-1), L0_ffn_route_id, L0_ffn_Wi, L0_ffn_bi, L0_ffn_Wr, L0_ffn_br, L0_ffn_Ws, L0_ffn_bs, L0_ffn_Wo, L0_ffn_bo)
    return h

_drawn_inputs = setup_inputs


def setup_inputs(seed=0):
    import zlib

    import numpy as np

    out = dict(_drawn_inputs(seed))
    spreads = {'L0_tok_b1': (0.0, 0.1),
     'L0_tok_ln_g': (1.0, 0.2),
     'L0_tok_ln_b': (0.0, 0.1),
     'L0_tok_b2': (0.0, 0.1),
     'L0_ffn_bi': (0.0, 0.667),
     'L0_ffn_bo': (0.0, 0.1)}
    factors = {'L0_ffn_Wi': 3.434,
     'L0_ffn_Wr': 7.959,
     'L0_ffn_br': 8.0,
     'L0_ffn_Ws': 8.0,
     'L0_ffn_bs': 8.0}
    for name, (base, spread) in spreads.items():
        noise = np.random.default_rng([zlib.crc32(name.encode()), seed]).standard_normal(out[name].shape)
        drawn = base * np.exp(spread * noise) if base else spread * noise
        out[name] = jnp.asarray(drawn.astype(out[name].dtype))
    for name, factor in factors.items():
        out[name] = (out[name] * factor).astype(out[name].dtype)
    return out
```

```python
from contextlib import ExitStack

import concourse.bass as bass
from concourse import mybir

ALU = mybir.AluOpType
ACT = mybir.ActivationFunctionType
AX = mybir.AxisListType
F32 = mybir.dt.float32
F16 = mybir.dt.float16
BF16 = mybir.dt.bfloat16
I32 = mybir.dt.int32
F32R = mybir.dt.float32r

B, T, D, H = 16, 1024, 64, 128
P = 128
NT = T // P
HALF = T // 2
NG = 4
GROUP = T // NG
E = 16
EROW = 2 * H + 2
CHUNK = 4
TABLE_STEPS = 2 + 3 + 4 * (E // CHUNK)
PARTS = 3
ROWS = 2 * PARTS * PARTS
EPS = 1e-5
TINY = 1e-30
PREP_FOLD = 8
GW_STEPS = 2 + 5 + 6 + 5
PREP_PARTS = 39
RSQRT_SEED = 1597463007.0


def tower(nc, x, w1, b1, ln_g, ln_b_col, w2, b2x2, route, wi_t, bi, experts, shared, wo_t, box2, row_mask, out):
    ctx = ExitStack()
    with ctx:
        def sb(name, shape, dt=F32):
            return ctx.enter_context(nc.sbuf_tensor(name, shape, dt))

        def sem(name):
            return ctx.enter_context(nc.semaphore(name))

        ident = sb("ident", [P, P])
        ident16 = sb("ident16", [P, P], F16)
        ones = sb("ones", [D, P])
        w1_sb = sb("w1_sb", [D, H])
        rows_sb = sb("rows_sb", [P, 2, H])
        ln_b_sb = sb("ln_b_sb", [H, 1])
        w2_sb = sb("w2_sb", [H, D])
        b2_sb = sb("b2_sb", [P, 1])
        wi_sb = sb("wi_sb", [P, H])
        wi_part = sb("wi_part", [P, 2, H], F32R)
        bi_sb = sb("bi_sb", [P, 1])
        wo_sb = sb("wo_sb", [H, D])
        bo_sb = sb("bo_sb", [P, 1])
        mask_sb = sb("mask_sb", [ROWS, 2 * PARTS])
        shared_sb = sb("shared_sb", [P, 1, EROW])
        table = sb("table", [P, 2, E + 1, 2 * H], F32R)
        table_b = sb("table_b", [P, E + 1, 2])
        route_i = sb("route_i", [1, B * NG], I32)
        route_f = sb("route_f", [1, 3, B * NG])
        route_e = sb("route_e", [1, B * NG], I32)

        select_at = nc.sbuf_base
        stage = sb("stage", [P, E * EROW])
        wsel = nc.alloc_sbuf_tensor_at("wsel", [P, 2, NG, 2, 2 * H], F32R, offset=select_at)
        x_sb = sb("x_sb", [P, P], I32)
        fold = sb("fold", [P, 3, H])
        fold2 = sb("fold2", [P, 3, H])
        stat = sb("stat", [P, 12])
        tok_a = sb("tok_a", [P, 3, P])
        tok_v = sb("tok_v", [P, P])
        tok_y = sb("tok_y", [P, 4, P])
        mr = sb("mr", [P, 2, P])
        mr_rest = sb("mr_rest", [P, 2, 2, P])
        mr_part = sb("mr_part", [P, PARTS, 2, P], BF16)
        gw = sb("gw", [P, 2, H])
        gw_rest = sb("gw_rest", [P, 2, 2, H])
        gw_part = sb("gw_part", [P, PARTS, 2, H], BF16)
        mlp_w = sb("mlp_w", [ROWS, H], BF16)
        mlp_terms = sb("mlp_terms", [ROWS, 2 * PARTS, H])
        shared_at = nc.sbuf_base
        sb("shared_place", [P, B * T], BF16)

        def at(name, shape, dt, offset):
            return nc.alloc_sbuf_tensor_at(name, shape, dt, offset=shared_at + offset)

        mlp_x = at("mlp_x", [ROWS, B * T], BF16, 0)
        h1 = at("h1", [P, T], F32, 0)
        h1_hi = at("h1_hi", [P, T], F32R, 4 * T)
        h1_lo = at("h1_lo", [P, T], F32R, 8 * T)
        h2 = at("h2", [P, T], F32, 12 * T)
        h2_hi = at("h2_hi", [P, T], F32R, 16 * T)
        h2_lo = at("h2_lo", [P, T], F32R, 20 * T)
        h3 = at("h3", [P, T], F32, 24 * T)
        h_t = sb("h_t", [P, 2, HALF])

        h_all = sb("h_all", [P, B * NT * D])

        probs = sb("probs", [P, 4, T])
        xn = sb("xn", [P, 2, NT * D])
        xc = sb("xc", [P, NT * D])
        xsq = sb("xsq", [P, NT * D])
        hl = sb("hl", [P, NT, 2 * D], F16)
        hi_lo = sb("hi_lo", [P, 2, T], F16)
        lo_hi = sb("lo_hi", [P, 2, T], F16)
        lnstat = sb("lnstat", [P, 2, 4, NT])
        minus_half = sb("minus_half", [P, NT])
        eps_sb = sb("eps_sb", [P, NT])
        denom = sb("denom", [P, 2, NT])
        rdenom = sb("rdenom", [P, NT])
        ctx_t = sb("ctx_t", [P, HALF])
        ctx_n = sb("ctx_n", [P, NT * D])
        h_mid = sb("h_mid", [P, 2, NT * D])

        yn = sb("yn", [P, NT * D])
        yc = sb("yc", [P, NT * D])
        ysq = sb("ysq", [P, NT * D])
        hl2 = sb("hl2", [P, NT, 2 * D], F16)
        hi_lo2 = sb("hi_lo2", [P, T], F32R)
        wsel_b = sb("wsel_b", [P, 2, NG, 2])
        y_t = sb("y_t", [P, HALF])
        y_out = sb("y_out", [P, 2, NT * D])

        ps_s = ctx.enter_context(nc.psum_tensor("ps_s", [P, 2, T], F32))
        ps_o = ctx.enter_context(nc.psum_tensor("ps_o", [P, HALF], F32))
        ps_a = ctx.enter_context(nc.psum_tensor("ps_a", [P, HALF], F32))
        ps_b = ctx.enter_context(nc.psum_tensor("ps_b", [P, HALF], F32))
        ps_c = ctx.enter_context(nc.psum_tensor("ps_c", [P, HALF], F32))

        staging = stage[:, :].rearrange("p (e r) -> p e r", r=EROW)
        scratch = nc.dram_tensor("mlp_rows", [2 * PARTS, B * T], BF16, kind="Internal").ap()

        s_load = {k: sem(f"s_load_{k}") for k in ("w1", "rows", "x", "w2", "ln_b", "route", "ffn", "table")}
        s_ident = sem("s_ident")
        s_ones = sem("s_ones")
        s_prep = sem("s_prep")
        s_usum = sem("s_usum")
        s_gw = sem("s_gw")
        s_scratch = sem("s_scratch")
        s_rows = [sem(f"s_rows{c}") for c in range(2)]
        s_route = sem("s_route")
        s_wi = sem("s_wi")
        s_table = sem("s_table")
        s_half = sem("s_half")
        s_hid = sem("s_hid")
        s_gelu = sem("s_gelu")
        s_w2 = sem("s_w2")
        s_ht = sem("s_ht")
        s_htt = sem("s_htt")
        s_h = sem("s_h")
        LN = ("sum", "cen", "sq", "ssq", "var", "rstd", "norm", "hi", "lo")
        n1 = {k: sem(f"s_n1_{k}") for k in LN}
        n2 = {k: sem(f"s_n2_{k}") for k in LN}
        s_xt = sem("s_xt")
        s_hilo = sem("s_hilo")
        s_swap = [sem(f"s_swap{i}") for i in range(2)]
        s_score = sem("s_score")
        s_exp = sem("s_exp")
        s_pv = sem("s_pv")
        s_ctx = sem("s_ctx")
        s_ctxt = sem("s_ctxt")
        s_rden = sem("s_rden")
        s_ctxn = sem("s_ctxn")
        s_res = sem("s_res")
        s_yt = sem("s_yt")
        s_hilo2 = sem("s_hilo2")
        s_in = sem("s_in")
        s_h1 = sem("s_h1")
        s_h1_hi = sem("s_h1_hi")
        s_h1_lo = sem("s_h1_lo")
        s_h2_hi = sem("s_h2_hi")
        s_h2_lo = sem("s_h2_lo")
        s_l1 = sem("s_l1")
        s_h2 = sem("s_h2")
        s_l2 = sem("s_l2")
        s_h3 = sem("s_h3")
        s_wo = sem("s_wo")
        s_y = sem("s_y")
        s_ytt = sem("s_ytt")
        s_out = sem("s_out")
        s_sel = [sem(f"s_sel{i}") for i in range(2)]
        s_store = [sem(f"s_store{i}") for i in range(2)]

        block = ctx.enter_context(nc.Block())

        def wait(eng, s, n):
            if not isinstance(n, int) or n > 0:
                eng.wait_ge(s, n)

        def pipeline(eng, turn, first, last):
            def whole(i):
                turn(i, i % 2, lambda d: 0 <= i + d < B)
            for i in range(first):
                whole(i)
            with eng.Fori(0, (last + 1 - first) // 2) as pair:
                turn(pair * 2 + first, first % 2, lambda d: True)
                turn(pair * 2 + (first + 1), (first + 1) % 2, lambda d: True)
            for i in range(last + 1, B + 2):
                whole(i)

        MLP_LOOP = (3, B - 8)
        MAIN_LOOP = (4, B - 3)
        CHUNKS = ((0, 2 * T), (2 * T, B * T))

        def tiles(ap):
            return ap.rearrange("p (k d) -> p k d", d=D)

        def halves(ap):
            return ap.rearrange("p (j f d) -> p f j d", f=2, d=D)

        def by_half(ap):
            return ap.rearrange("p (f j d) -> p f j d", f=2, d=D)

        def over_d(ap):
            return ap.unsqueeze(2).to_broadcast([P, NT, D])

        def batch(ap, i, n=NT * D):
            return ap[:, bass.ts(i, n)]

        @block.sync
        def _(sp):
            sp.dma_start(w1_sb[:, :], w1).then_inc(s_load["w1"], 16)
            sp.dma_start(rows_sb[:, 0, :], b1.partition_broadcast(P)).then_inc(s_load["rows"], 16)
            sp.dma_start(mask_sb[:, :], row_mask).then_inc(s_load["rows"], 16)
            sp.dma_start(w2_sb[:, :], w2).then_inc(s_load["w2"], 16)
            sp.dma_start(b2_sb[:, :], b2x2).then_inc(s_load["w2"], 16)
            sp.wait_ge(s_prep, PREP_PARTS)
            sp.dma_start(scratch.rearrange("(n k) (p f) -> p n k f", k=2, f=P), mr_part[:, :, :, :])\
              .then_inc(s_scratch, 16)
            sp.wait_ge(s_scratch, 16)
            for c, (a, z) in enumerate(CHUNKS):
                sp.dma_start(mlp_x[:, a:z], scratch[:, a:z].unsqueeze(0).to_broadcast([PARTS, 2 * PARTS, z - a]))\
                  .then_inc(s_rows[c], 16)

            def swap(b, q):
                wait(sp, s_hilo, b + 1)
                wait(sp, s_score, 8 * (b - 1))
                sp.dma_start(lo_hi[0:D, q, :], hi_lo[D:P, q, :]).then_inc(s_swap[q], 16)
                sp.dma_start(lo_hi[D:P, q, :], hi_lo[0:D, q, :]).then_inc(s_swap[q], 16)

            swap(0, 0)
            sp.wait_ge(s_route, 6)
            sp.wait_ge(s_table, TABLE_STEPS)

            def turn(i, q, has):
                if has(-1):
                    b = i - 1
                    wait(sp, s_h3, 4 * (b - 1))
                    for g in range(NG):
                        e = sp.value_load(route_e[0:1, bass.ds(b * NG + g, 1)], min_val=0, max_val=E)
                        sp.dma_start(wsel[:, 1 - q, g, :, :].bitcast(F32), table[:, :, bass.ds(e, 1), :].bitcast(F32)).then_inc(s_sel[1 - q], 16)
                        sp.dma_start(wsel_b[:, 1 - q, g, :], table_b[:, bass.ds(e, 1), :]).then_inc(s_sel[1 - q], 16)
                if has(1):
                    swap(i + 1, 1 - q)
                if has(-2):
                    b = i - 2
                    wait(sp, s_out, b + 1)
                    sp.dma_start(out[bass.ds(b, 1), :, :].rearrange("o (k p) d -> p (o k) d", p=P),
                                 tiles(y_out[:, q, :])).then_inc(s_store[q], 16)

            pipeline(sp, turn, *MAIN_LOOP)
            for q in range(2):
                sp.wait_ge(s_store[q], 16 * B // 2)

        @block.gpsimd
        def _(pool):
            pool.memset(ident[:, :], 0.0).then_inc(s_ident, 1)
            pool.memset(ident16[:, :], 0.0).then_inc(s_ident, 1)
            pool.wait_ge(s_ident, 2)
            for m in (ident, ident16):
                pool.affine_select(out=m[:, :], in_=m[:, :], compare_op=ALU.not_equal, fill=1.0, base=0,
                                   pattern=[[-1, P]], channel_multiplier=1).then_inc(s_ident, 1)
            pool.memset(minus_half[:, :], -0.5).then_inc(s_half, 1)
            pool.memset(eps_sb[:, :], EPS).then_inc(s_half, 1)
            steps = [0]

            def step(ins):
                steps[0] += 1
                ins.then_inc(s_gw, 1)
                pool.wait_ge(s_gw, steps[0])

            pool.wait_ge(s_load["rows"], 16 * 3)
            pool.dma_start(staging, experts).then_inc(s_load["table"], 16)
            pool.dma_start(shared_sb[:, 0, :], shared).then_inc(s_load["table"], 16)
            pool.wait_ge(s_prep, PREP_FOLD)
            for n in range(2):
                step(pool.tensor_tensor(gw[:, n, :], fold[:, n, :], rows_sb[:, 1, :], ALU.mult))
            src = gw[:, :, :]
            for n in range(PARTS):
                step(pool.tensor_copy(gw_part[:, n], src))
                if n < PARTS - 1:
                    step(pool.tensor_tensor(gw_rest[:, n], src, gw_part[:, n], ALU.subtract))
                    src = gw_rest[:, n]
            for v in range(2):
                for n in range(PARTS):
                    t = PARTS * v + n
                    step(pool.tensor_tensor(mlp_terms[:, t, :], gw_part[0:ROWS, n, v, :],
                                            mask_sb[:, t:t + 1].to_broadcast([ROWS, H]), ALU.mult))
            acc = mlp_terms[:, 0, :]
            for t in range(1, 2 * PARTS):
                to = mlp_w[:, :] if t == 2 * PARTS - 1 else mlp_terms[:, t, :]
                step(pool.tensor_tensor(to, acc, mlp_terms[:, t, :], ALU.add))
                acc = mlp_terms[:, t, :]
            assert steps[0] == GW_STEPS

            pool.wait_ge(s_load["table"], 32)
            pool.wait_ge(s_ident, 4)
            made = [0]

            def entry(ins, chained=True):
                made[0] += 1
                ins.then_inc(s_table, 1)
                if chained:
                    pool.wait_ge(s_table, made[0])

            for n in range(2):
                m = shared_sb[:, 0, n * H:(n + 1) * H]
                entry(pool.tensor_tensor(m, m, ident[:, :], ALU.add))
            w = shared_sb[:, :, 0:2 * H]
            entry(pool.tensor_copy(table[:, 0, E:E + 1, :], w))
            entry(pool.tensor_tensor(table[:, 1, E:E + 1, :], w, table[:, 0, E:E + 1, :].bitcast(F32), ALU.subtract))
            entry(pool.tensor_copy(table_b[:, E:E + 1, :], shared_sb[:, :, 2 * H:]))
            for n in range(0, E, CHUNK):
                m = staging[:, n:n + CHUNK, :]
                entry(pool.tensor_tensor(m, m, shared_sb[:, :, :].to_broadcast([P, CHUNK, EROW]), ALU.add))
                w, hi = m[:, :, 0:2 * H], table[:, 0, n:n + CHUNK, :]
                entry(pool.tensor_copy(hi, w))
                entry(pool.tensor_tensor(table[:, 1, n:n + CHUNK, :], w, hi.bitcast(F32), ALU.subtract))
                entry(pool.tensor_copy(table_b[:, n:n + CHUNK, :], m[:, :, 2 * H:]))
            assert made[0] <= TABLE_STEPS, made[0]

            def rstd(n, s, b):
                wait(pool, s["ssq"], b + 1)
                wait(pool, s["norm"], b)
                pool.tensor_tensor(lnstat[:, n, 2, :], lnstat[:, n, 1, :], eps_sb[:, :], ALU.add)\
                    .then_inc(s["var"], 1)
                wait(pool, s["var"], b + 1)
                pool.tensor_tensor(lnstat[:, n, 3, :], lnstat[:, n, 2, :], minus_half[:, :], ALU.pow)\
                    .then_inc(s["rstd"], 1)

            def low(s, x_n, x_hl, b):
                wait(pool, s["hi"], b + 1)
                pool.tensor_tensor(x_hl[:, :, D:2 * D], tiles(x_n), x_hl[:, :, 0:D], ALU.subtract)\
                    .then_inc(s["lo"], 1)

            pool.wait_ge(s_half, 2)
            rstd(0, n1, 0)
            low(n1, xn[:, 0, :], hl, 0)
            rstd(0, n1, 1)

            def turn(i, q, has):
                if has(1):
                    low(n1, xn[:, 1 - q, :], hl, i + 1)
                if has(-1):
                    rstd(1, n2, i - 1)
                    low(n2, yn[:, :], hl2, i - 1)
                if has(2):
                    rstd(0, n1, i + 2)

            pipeline(pool, turn, *MAIN_LOOP)

        @block.tensor
        def _(pe):
            pe.wait_ge(s_load["w1"], 16)
            pe.wait_ge(s_ones, 1)
            pe.matmul(ps_a[:, 0:H], ones[:, :], w1_sb[:, :], start=True, stop=True).then_inc(s_usum, 1)
            pe.wait_ge(s_gw, GW_STEPS)
            pe.wait_ge(s_ident, 4)
            pe.wait_ge(s_load["w2"], 32)
            hid = (ps_o, ps_a)
            tps = (ps_b, ps_c)

            def x_transposes(b, bank):
                wait(pe, n1["lo"], b + 1)
                for k in range(NT):
                    m = pe.transpose(bank.bitcast(F16)[:, k * P:(k + 1) * P], hl[:, k, :], ident16[:, :])
                m.then_inc(s_xt, 1)

            def mlp_turn(i, q, has):
                if has(0):
                    for c in range(2):
                        if isinstance(i, int) and i == CHUNKS[c][0] // T:
                            pe.wait_ge(s_rows[c], 16)
                    wait(pe, s_gelu, i - 1)
                    for f in range(2):
                        m = pe.matmul(ps_s[:, q, f * HALF:(f + 1) * HALF], mlp_w[:, :],
                                      mlp_x[:, bass.ds(i * T + f * HALF, HALF)], start=True, stop=True)
                    m.then_inc(s_hid, 1)
                if has(-1):
                    b = i - 1
                    wait(pe, s_gelu, b + 1)
                    wait(pe, s_ht, b - 1)
                    for f in range(2):
                        m = pe.matmul(hid[1 - q][f * D:(f + 1) * D, :], w2_sb[:, :],
                                      probs[:, 1 - q, f * HALF:(f + 1) * HALF], start=True, stop=True)
                    m.then_inc(s_w2, 1)
                if has(-2):
                    b = i - 2
                    wait(pe, s_ht, b + 1)
                    wait(pe, s_h, b - 1)
                    for j in range(NT // 2):
                        m = pe.transpose(tps[q][:, j * P:(j + 1) * P], h_t[:, q, j * P:(j + 1) * P], ident[:, :])
                    m.then_inc(s_htt, 1)
                if isinstance(i, int) and i == B - 1:
                    x_transposes(0, ps_s[:, 0, 0:HALF])

            pipeline(pe, mlp_turn, *MLP_LOOP)

            def scores(i, q, g):
                if g == 0:
                    wait(pe, s_hilo, i + 1)
                    pe.wait_ge(s_swap[q], (i - q) * 16 + 32)
                for c in (2 * g, 2 * g + 1):
                    wait(pe, s_exp, 8 * i + c - 1)
                    for f in range(2):
                        o = ps_s[:, c % 2, f * HALF:(f + 1) * HALF]
                        k = hi_lo[:, q, c * P:(c + 1) * P]
                        pe.matmul(o, k, hi_lo[:, q, f * HALF:(f + 1) * HALF], start=True, stop=False)
                        m = pe.matmul(o, k, lo_hi[:, q, f * HALF:(f + 1) * HALF], start=False, stop=True)
                    m.then_inc(s_score, 1)

            def context(i, q, g):
                if g == 0:
                    wait(pe, s_ctx, i)
                for c in (2 * g, 2 * g + 1):
                    wait(pe, s_exp, 8 * i + c + 1)
                    for f in range(2):
                        m = pe.matmul(ps_o[f * D:(f + 1) * D, :], xn[:, q, c * D:(c + 1) * D],
                                      probs[:, c % 4, f * HALF:(f + 1) * HALF], start=(c == 0), stop=(c == NT - 1))
                    m.then_inc(s_pv, 1)

            def layer(b, q, n, hi_there, lo_there, x_hi, x_lo, done):
                for f, bank in enumerate((ps_a, ps_b)):
                    wait(pe, hi_there, 2 * b + f + 1)
                    wait(pe, lo_there, 2 * b + f + 1)
                    for g in (2 * f, 2 * f + 1):
                        o = bank[:, (g % 2) * GROUP:(g % 2 + 1) * GROUP]
                        hi, lo = (x[:, g * GROUP:(g + 1) * GROUP] for x in (x_hi, x_lo))
                        w_hi, w_lo = (wsel[:, q, g, t, n * H:(n + 1) * H] for t in range(2))
                        pe.matmul(o, w_hi, hi, start=True, stop=False)
                        pe.matmul(o, w_lo, hi, start=False, stop=False)
                        m = pe.matmul(o, w_hi, lo, start=False, stop=True)
                    m.then_inc(done, 1)

            def turn(i, q, has):
                b = i - 2
                if has(0):
                    scores(i, q, 0)
                if has(-1):
                    context(i - 1, 1 - q, 3)
                if has(-2):
                    wait(pe, s_sel[q], (b - q) * 64 + 128)
                    layer(b, q, 0, s_h1_hi, s_h1_lo, h1_hi, h1_lo, s_l1)
                if has(-1):
                    wait(pe, s_ctx, i)
                    for j in range(NT // 2):
                        m = pe.transpose(ps_c[:, j * P:(j + 1) * P], ctx_t[:, j * P:(j + 1) * P], ident[:, :])
                    m.then_inc(s_ctxt, 1)
                if has(0):
                    scores(i, q, 1)
                if has(-2):
                    layer(b, q, 1, s_h2_hi, s_h2_lo, h2_hi, h2_lo, s_l2)
                if has(0):
                    context(i, q, 0)
                if has(-2):
                    for f in range(2):
                        wait(pe, s_h3, 4 * b + 2 * f + 2)
                        m = pe.matmul(ps_a[f * D:(f + 1) * D, :], wo_sb[:, :], h3[:, f * HALF:(f + 1) * HALF],
                                      start=True, stop=True)
                    m.then_inc(s_wo, 1)
                if has(0):
                    scores(i, q, 2)
                if has(1):
                    wait(pe, s_ctxn, i)
                    x_transposes(i + 1, ps_c[:, :])
                if has(-2):
                    wait(pe, s_y, b + 1)
                    for j in range(NT // 2):
                        m = pe.transpose(ps_b[:, j * P:(j + 1) * P], y_t[:, j * P:(j + 1) * P], ident[:, :])
                    m.then_inc(s_ytt, 1)
                if has(0):
                    context(i, q, 1)
                if has(0):
                    scores(i, q, 3)
                if has(-1):
                    c = i - 1
                    wait(pe, n2["lo"], c + 1)
                    for k in range(NT):
                        m = pe.transpose(ps_a[:, :].bitcast(F16)[:, k * P:(k + 1) * P], hl2[:, k, :], ident16[:, :])
                    m.then_inc(s_yt, 1)
                if has(0):
                    context(i, q, 2)
                if has(-1):
                    wait(pe, s_hilo2, c + 1)
                    wait(pe, s_out, c)
                    wait(pe, s_hilo, min(i + 2, B) if isinstance(i, int) else i + 2)
                    if isinstance(i, int) and i == 1:
                        pe.wait_ge(s_wi, 3)
                        pe.wait_ge(s_load["ffn"], 16 * 5)
                    for f, bank in enumerate((ps_b, ps_c)):
                        for n in range(2):
                            m = pe.matmul(bank[:, :], wi_part[:, n, :], hi_lo2[:, f * HALF:(f + 1) * HALF],
                                          start=(n == 0), stop=(n == 1))
                        m.then_inc(s_in, 1)

            pipeline(pe, turn, *MAIN_LOOP)

        @block.scalar
        def _(act):
            act.dma_start(x_sb[:, :], x.rearrange("b (q f) -> (b q) f", f=P)).then_inc(s_load["x"], 16)
            act.dma_start(rows_sb[:, 1, :], ln_g.partition_broadcast(P)).then_inc(s_load["rows"], 16)
            act.dma_start(ln_b_sb[:, :], ln_b_col).then_inc(s_load["ln_b"], 16)
            act.dma_start(route_i[:, :], route).then_inc(s_load["route"], 16)
            act.dma_start(wi_sb[0:D, :], wi_t).then_inc(s_load["ffn"], 16)
            act.dma_start(wi_sb[D:P, :], wi_t).then_inc(s_load["ffn"], 16)
            act.dma_start(bi_sb[:, :], bi).then_inc(s_load["ffn"], 16)
            act.dma_start(wo_sb[:, :], wo_t).then_inc(s_load["ffn"], 16)
            act.dma_start(bo_sb[:, :], box2).then_inc(s_load["ffn"], 16)
            act.wait_ge(s_load["ln_b"], 16)

            def mlp_turn(i, q, has):
                if has(0):
                    wait(act, s_hid, i + 1)
                    wait(act, s_w2, i - 1)
                    act.activation(probs[:, q, :], ps_s[:, q, :], ACT.Gelu, bias=ln_b_sb[:, :]).then_inc(s_gelu, 1)
                if isinstance(i, int) and i == B - 5:
                    square(n1, xsq, xc, 0)
                if isinstance(i, int) and i == B - 1:
                    square(n1, xsq, xc, 1)

            def square(s, dst, src, b):
                wait(act, s["cen"], b + 1)
                wait(act, s["ssq"], b)
                act.activation(dst[:, :], src[:, :], ACT.Square, scale=float(D) ** -0.5).then_inc(s["sq"], 1)

            pipeline(act, mlp_turn, *MLP_LOOP)
            act.wait_ge(s_w2, B)

            def exps(i, q, g):
                for c in (2 * g, 2 * g + 1):
                    if c == 0:
                        wait(act, s_rden, i - 1)
                    wait(act, s_score, 8 * i + c + 1)
                    wait(act, s_pv, 8 * i + c - 3)
                    act.activation(probs[:, c % 4, :], ps_s[:, c % 2, :], ACT.Exp, scale=float(D) ** -0.5,
                                   accum_out=denom[:, q, c:c + 1]).then_inc(s_exp, 1)

            def relus(i, q, n, dst, src_done, read, per, done):
                b = i - 2
                for g in range(NG):
                    if g % 2 == 0:
                        wait(act, src_done, 2 * b + g // 2 + 1)
                    if g == 0:
                        wait(act, read, per * b)
                        wait(act, s_sel[q], (b - q) * 64 + 128)
                    bank = (ps_a, ps_b)[g // 2]
                    act.activation(dst[:, g * GROUP:(g + 1) * GROUP], bank[:, (g % 2) * GROUP:(g % 2 + 1) * GROUP],
                                   ACT.Relu, bias=wsel_b[:, q, g, n:n + 1]).then_inc(done, 1)

            def turn(i, q, has):
                if has(0):
                    exps(i, q, 0)
                if has(-2):
                    relus(i, q, 0, h2, s_l1, s_h2_lo, 2, s_h2)
                if has(0):
                    exps(i, q, 1)
                if has(-2):
                    relus(i, q, 1, h3, s_l2, s_wo, 1, s_h3)
                if has(-1):
                    square(n2, ysq, yc, i - 1)
                if has(0):
                    exps(i, q, 2)
                if has(2):
                    square(n1, xsq, xc, i + 2)
                if has(0):
                    exps(i, q, 3)

            pipeline(act, turn, *MAIN_LOOP)

        @block.vector
        def _(dve):
            done = [0]

            def step(ins):
                done[0] += 1
                ins.then_inc(s_prep, 1)
                dve.wait_ge(s_prep, done[0])

            dve.memset(ones[:, :], 1.0).then_inc(s_ones, 1)
            dve.wait_ge(s_load["x"], 16)
            step(dve.tensor_scalar(tok_a[:, 0, :], x_sb[:, :], 1.0 / 127.5, -1.0, ALU.mult, ALU.add))
            step(dve.tensor_scalar(tok_a[:, 1, :], tok_a[:, 0, :], -1.0, None, ALU.mult))
            step(dve.tensor_tensor(tok_a[:, 2, :], tok_a[:, 0, :], tok_a[:, 1, :], ALU.max))
            dve.wait_ge(s_load["rows"], 16 * 3)
            dve.wait_ge(s_usum, 1)
            step(dve.tensor_reduce(stat[:, 0:1], ps_a[:, 0:H], AX.X, ALU.add))
            step(dve.tensor_reduce(stat[:, 1:2], rows_sb[:, 0, :], AX.X, ALU.add))
            step(dve.tensor_scalar(stat[:, 2:4], stat[:, 0:2], 1.0 / H, None, ALU.mult))
            step(dve.tensor_scalar(fold[:, 0, :], ps_a[:, 0:H], stat[:, 2:3], None, ALU.subtract))
            step(dve.tensor_scalar(fold[:, 1, :], rows_sb[:, 0, :], stat[:, 3:4], None, ALU.subtract))
            for n in range(2):
                step(dve.tensor_tensor(fold2[:, n, :], fold[:, n, :], fold[:, 0, :], ALU.mult))
            step(dve.tensor_reduce(stat[:, 4:6], fold2[:, 0:2, :], AX.X, ALU.add))
            step(dve.tensor_scalar(stat[:, 6:7], stat[:, 4:5], TINY, None, ALU.max))
            step(dve.reciprocal(stat[:, 7:8], stat[:, 6:7]))
            step(dve.tensor_tensor(stat[:, 8:9], stat[:, 5:6], stat[:, 7:8], ALU.mult))
            step(dve.tensor_scalar(fold2[:, 2, :], fold[:, 0, :], stat[:, 8:9], None, ALU.mult))
            step(dve.tensor_tensor(fold[:, 2, :], fold[:, 1, :], fold2[:, 2, :], ALU.subtract))
            step(dve.tensor_tensor(fold2[:, 2, :], fold[:, 2, :], fold[:, 2, :], ALU.mult))
            step(dve.tensor_reduce(stat[:, 9:10], fold2[:, 2, :], AX.X, ALU.add))
            step(dve.tensor_scalar(stat[:, 10:11], stat[:, 9:10], 1.0 / H, EPS, ALU.mult, ALU.add))
            step(dve.tensor_scalar(stat[:, 0:1], stat[:, 4:5], 1.0 / H, None, ALU.mult))
            step(dve.tensor_scalar(tok_y[:, 0, :], tok_a[:, 2, :], stat[:, 8:9], None, ALU.add))
            step(dve.scalar_tensor_tensor(tok_y[:, 1, :], tok_y[:, 0, :], stat[:, 0:1], tok_y[:, 0, :],
                                          ALU.mult, ALU.mult))
            step(dve.tensor_scalar(tok_v[:, :], tok_y[:, 1, :], stat[:, 10:11], None, ALU.add))
            step(dve.tensor_scalar(tok_y[:, 0, :].bitcast(I32), tok_v[:, :].bitcast(I32), -0.5, RSQRT_SEED,
                                   ALU.mult, ALU.add))
            for n in range(3):
                y, y_next = tok_y[:, n % 2, :], (tok_y[:, (n + 1) % 2, :] if n < 2 else mr[:, 1, :])
                step(dve.scalar_tensor_tensor(tok_y[:, 2, :], y, -0.5, y, ALU.mult, ALU.mult))
                step(dve.tensor_tensor(tok_y[:, 3, :], tok_y[:, 2, :], tok_v[:, :], ALU.mult))
                step(dve.scalar_tensor_tensor(y_next, tok_y[:, 3, :], 1.5, y, ALU.add, ALU.mult))
            step(dve.tensor_tensor(mr[:, 0, :], tok_a[:, 2, :], mr[:, 1, :], ALU.mult))

            def split(parts, whole, rest):
                src = whole
                for n in range(PARTS):
                    step(dve.tensor_copy(parts[n], src))
                    if n < PARTS - 1:
                        step(dve.tensor_tensor(rest[n], src, parts[n], ALU.subtract))
                        src = rest[n]

            split([mr_part[:, n] for n in range(PARTS)], mr[:, :, :], [mr_rest[:, n] for n in range(2)])
            assert done[0] == PREP_PARTS, done[0]
            dve.wait_ge(s_load["route"], 16)
            dve.tensor_scalar(route_f[:, 0, :], route_i[:, :], -float(E), None, ALU.add).then_inc(s_route, 1)
            dve.tensor_scalar(route_f[:, 1, :], route_i[:, :], 0.0, None, ALU.is_ge).then_inc(s_route, 1)
            dve.wait_ge(s_route, 2)
            dve.scalar_tensor_tensor(route_f[:, 2, :], route_i[:, :], float(E - 1), route_f[:, 1, :],
                                     ALU.is_le, ALU.mult).then_inc(s_route, 1)
            dve.wait_ge(s_route, 3)
            dve.tensor_tensor(route_f[:, 1, :], route_f[:, 0, :], route_f[:, 2, :], ALU.mult).then_inc(s_route, 1)
            dve.wait_ge(s_route, 4)
            dve.tensor_scalar(route_e[:, :], route_f[:, 1, :], float(E), None, ALU.add).then_inc(s_route, 2)
            dve.wait_ge(s_load["ffn"], 16 * 5)
            dve.tensor_copy(wi_part[:, 0, :], wi_sb[:, :]).then_inc(s_wi, 1)
            dve.wait_ge(s_wi, 1)
            dve.tensor_tensor(wi_part[:, 1, :], wi_sb[:, :], wi_part[:, 0, :].bitcast(F32), ALU.subtract)\
               .then_inc(s_wi, 2)

            hid = (ps_o, ps_a)
            tps = (ps_b, ps_c)

            def mlp_turn(i, q, has):
                if has(-1):
                    b = i - 1
                    wait(dve, s_w2, b + 1)
                    wait(dve, s_htt, b - 1)
                    dve.tensor_scalar(h_t[:, 1 - q, :], hid[1 - q][:, :], b2_sb[:, :], None, ALU.add)\
                       .then_inc(s_ht, 1)
                if has(-2):
                    b = i - 2
                    wait(dve, s_htt, b + 1)
                    dve.tensor_copy(by_half(batch(h_all, b)), halves(tps[q][:, :])).then_inc(s_h, 1)
                if isinstance(i, int) and i == B - 6:
                    dve.wait_ge(s_h, 1)
                    centre(0, n1, 0, batch(h_all, 0), xc)
                if isinstance(i, int) and i == B - 4:
                    squares(0, n1, 0, xsq)
                if isinstance(i, int) and i == B - 3:
                    norm(0, n1, 0, xc, xn[:, 0, :], hl)
                if isinstance(i, int) and i == B - 2:
                    dve.wait_ge(n1["norm"], 1)
                    centre(0, n1, 1, batch(h_all, 1), xc)
                if isinstance(i, int) and i == B - 1:
                    x_out(0, 0, ps_s[:, 0, 0:HALF])
                if isinstance(i, int) and i == B:
                    squares(0, n1, 1, xsq)

            def centre(n, s, b, x, x_c):
                dve.tensor_reduce(lnstat[:, n, 0, :], tiles(x), AX.X, ALU.add).then_inc(s["sum"], 1)
                wait(dve, s["sum"], b + 1)
                dve.scalar_tensor_tensor(tiles(x_c[:, :]), over_d(lnstat[:, n, 0, :]), -1.0 / D,
                                         tiles(x), ALU.mult, ALU.add).then_inc(s["cen"], 1)

            def squares(n, s, b, x_sq):
                wait(dve, s["sq"], b + 1)
                wait(dve, s["var"], b)
                dve.tensor_reduce(lnstat[:, n, 1, :], tiles(x_sq[:, :]), AX.X, ALU.add).then_inc(s["ssq"], 1)

            def norm(n, s, b, x_c, x_n, x_hl):
                wait(dve, s["rstd"], b + 1)
                dve.tensor_tensor(tiles(x_n), tiles(x_c[:, :]), over_d(lnstat[:, n, 3, :]), ALU.mult)\
                   .then_inc(s["norm"], 1)
                wait(dve, s["norm"], b + 1)
                dve.tensor_copy(x_hl[:, :, 0:D], tiles(x_n)).then_inc(s["hi"], 1)

            def x_out(b, q, bank):
                wait(dve, s_xt, b + 1)
                wait(dve, s_score, 8 * (b - 1))
                if not isinstance(b, int) or b >= 2:
                    dve.wait_ge(s_swap[q], (b - q) * 16)
                dve.tensor_copy(hi_lo[:, q, :], bank.bitcast(F16)).then_inc(s_hilo, 1)

            dve.wait_ge(s_load["w2"], 32)
            pipeline(dve, mlp_turn, *MLP_LOOP)
            dve.wait_ge(s_h, B)

            def parts(b, f, src, hi, lo, there, per, read, hi_done, lo_done):
                h = slice(f * HALF, (f + 1) * HALF)
                wait(dve, there, per * b + (f + 1) * per // 2)
                wait(dve, read, 2 * b)
                dve.tensor_copy(hi[:, h], src[:, h]).then_inc(hi_done, 1)
                wait(dve, hi_done, 2 * b + f + 1)
                dve.tensor_tensor(lo[:, h], src[:, h], hi[:, h].bitcast(F32), ALU.subtract).then_inc(lo_done, 1)

            def turn(i, q, has):
                b = i - 1
                if has(-1):
                    wait(dve, s_pv, 8 * (b + 1))
                    wait(dve, s_ctxt, b)
                    dve.tensor_copy(ctx_t[:, :], ps_o[:, :]).then_inc(s_ctx, 1)
                if has(1):
                    wait(dve, s_xt, i + 1)
                    norm(0, n1, i + 1, xc, xn[:, 1 - q, :], hl)
                if has(-2):
                    for f in range(2):
                        parts(i - 2, f, h2, h2_hi, h2_lo, s_h2, 4, s_l2, s_h2_hi, s_h2_lo)
                if has(-1):
                    wait(dve, s_exp, 8 * (b + 1))
                    dve.reciprocal(rdenom[:, :], denom[:, 1 - q, :]).then_inc(s_rden, 1)
                    wait(dve, s_rden, b + 1)
                    wait(dve, s_ctxt, b + 1)
                    rd = rdenom[:, :].rearrange("p (f j) -> p f j", f=2).unsqueeze(3).to_broadcast([P, 2, NT // 2, D])
                    dve.tensor_tensor(by_half(ctx_n[:, :]), halves(ps_c[:, :]), rd, ALU.mult).then_inc(s_ctxn, 1)
                    wait(dve, s_ctxn, b + 1)
                    dve.tensor_tensor(h_mid[:, 1 - q, :], batch(h_all, b), ctx_n[:, :], ALU.add).then_inc(s_res, 1)
                    wait(dve, s_res, b + 1)
                    centre(1, n2, b, h_mid[:, 1 - q, :], yc)
                if has(-1):
                    squares(1, n2, b, ysq)
                if has(-2):
                    wait(dve, s_wo, i - 1)
                    wait(dve, s_ytt, i - 2)
                    dve.tensor_scalar(y_t[:, :], ps_a[:, :], bo_sb[:, :], None, ALU.add).then_inc(s_y, 1)
                if has(2):
                    wait(dve, n1["norm"], i + 2)
                    centre(0, n1, i + 2, batch(h_all, i + 2), xc)
                if has(1):
                    x_out(i + 1, 1 - q, ps_c[:, :])
                if has(-1):
                    norm(1, n2, b, yc, yn[:, :], hl2)
                if has(2):
                    squares(0, n1, i + 2, xsq)
                if has(-2):
                    c = i - 2
                    wait(dve, s_ytt, c + 1)
                    if not isinstance(c, int) or c >= 2:
                        dve.wait_ge(s_store[q], (c - q) * 8)
                    dve.tensor_tensor(by_half(y_out[:, q, :]), halves(ps_b[:, :]), by_half(h_mid[:, q, :]), ALU.add)\
                       .then_inc(s_out, 1)
                if has(-1):
                    wait(dve, s_yt, b + 1)
                    wait(dve, s_in, 2 * b)
                    dve.tensor_copy(hi_lo2[:, :], ps_a[:, :].bitcast(F16)).then_inc(s_hilo2, 1)
                    for f, bank in enumerate((ps_b, ps_c)):
                        wait(dve, s_in, 2 * b + f + 1)
                        wait(dve, s_h1_lo, 2 * b)
                        dve.tensor_scalar(h1[:, f * HALF:(f + 1) * HALF], bank[:, :], bi_sb[:, :], 0.0,
                                          ALU.add, ALU.max).then_inc(s_h1, 1)
                        parts(b, f, h1, h1_hi, h1_lo, s_h1, 2, s_l1, s_h1_hi, s_h1_lo)

            pipeline(dve, turn, *MAIN_LOOP)


def kernel(x, L0_tok_W1, L0_tok_b1, L0_tok_ln_g, L0_tok_ln_b, L0_tok_W2, L0_tok_b2, L0_ffn_route_id,
           L0_ffn_Wi, L0_ffn_bi, L0_ffn_Wr, L0_ffn_br, L0_ffn_Ws, L0_ffn_bs, L0_ffn_Wo, L0_ffn_bo):
    import numpy as np
    import concourse.bacc as bacc
    from concourse.bass_utils import run_bass_kernel_spmd

    def col(v):
        return np.asarray(v).reshape(-1, 1)

    row_mask = np.zeros((ROWS, 2 * PARTS), np.float32)
    for r in range(ROWS):
        row_mask[r, PARTS * (r % 2) + r // (2 * PARTS)] = 1.0
    wr = np.transpose(np.asarray(L0_ffn_Wr), (3, 1, 0, 2)).reshape(H, E, 2 * H)
    br = np.transpose(np.asarray(L0_ffn_br), (2, 1, 0))
    ws = np.transpose(np.asarray(L0_ffn_Ws)[:, 0], (2, 0, 1)).reshape(H, 2 * H)
    bs = np.transpose(np.asarray(L0_ffn_bs)[:, 0], (1, 0))
    arrays = {
        "x": np.asarray(x),
        "w1": np.asarray(L0_tok_W1),
        "b1": np.asarray(L0_tok_b1),
        "ln_g": np.asarray(L0_tok_ln_g),
        "ln_b_col": col(L0_tok_ln_b),
        "w2": np.asarray(L0_tok_W2),
        "b2x2": col(np.concatenate([L0_tok_b2, L0_tok_b2])),
        "route": np.asarray(L0_ffn_route_id).reshape(1, -1),
        "wi_t": np.asarray(L0_ffn_Wi).T,
        "bi": col(L0_ffn_bi),
        "experts": np.concatenate([wr, br], axis=2),
        "shared": np.concatenate([ws, bs], axis=1),
        "wo_t": np.asarray(L0_ffn_Wo).T,
        "box2": col(np.concatenate([L0_ffn_bo, L0_ffn_bo])),
        "row_mask": row_mask,
    }
    nc = bacc.Bacc("TRN2", target_bir_lowering=False, num_devices=1)
    given, args = {}, []
    for name, a in arrays.items():
        a = np.ascontiguousarray(a)
        given[f"in_{name}"] = a
        args.append(nc.dram_tensor(f"in_{name}", a.shape, mybir.dt.from_np(a.dtype), kind="ExternalInput").ap())
    args.append(nc.dram_tensor("out_h", (B, T, D), F32, kind="ExternalOutput").ap())
    tower(nc, *args)
    r = run_bass_kernel_spmd(nc, [given], core_ids=[0])
    return r.results[0]["out_h"]
```

```python
from contextlib import ExitStack

import concourse.bass as bass
from concourse import mybir

ALU = mybir.AluOpType
ACT = mybir.ActivationFunctionType
AX = mybir.AxisListType
F32 = mybir.dt.float32
F16 = mybir.dt.float16
BF16 = mybir.dt.bfloat16
I32 = mybir.dt.int32
F32R = mybir.dt.float32r

B, T, D, H = 16, 1024, 64, 128
P = 128
NT = T // P
HALF = T // 2
NG = 4
GROUP = T // NG
E = 16
EROW = 2 * H + 2
CHUNK = 4
TABLE_STEPS = 2 + 3 + 4 * (E // CHUNK)
PARTS = 3
ROWS = 2 * PARTS * PARTS
EPS = 1e-5
TINY = 1e-30
PREP_FOLD = 5
GW_STEPS = 1 + 2 + 5
PREP_PARTS = 34
RSQRT_SEED = 1597463007.0


def tower(nc, x, w1, b1, ln_g, ln_b_col, w2, b2x2, route, wi_t, bi, experts, shared, wo_t, box2, row_mask, out):
    ctx = ExitStack()
    with ctx:
        def sb(name, shape, dt=F32):
            return ctx.enter_context(nc.sbuf_tensor(name, shape, dt))

        def sem(name):
            return ctx.enter_context(nc.semaphore(name))

        def next_place():
            return -(-nc.sbuf_base // 32) * 32

        select_at = next_place()
        stage = sb("stage", [P, E * EROW])
        wsel = nc.alloc_sbuf_tensor_at("wsel", [P, 2, NG, 2, 2 * H], F32R, offset=select_at)
        shared_at = next_place()
        sb("shared_place", [P, B * T], BF16)

        def at(name, shape, dt, offset):
            return nc.alloc_sbuf_tensor_at(name, shape, dt, offset=shared_at + offset)

        mlp_x = at("mlp_x", [ROWS, B * T], BF16, 0)
        h1 = at("h1", [P, T], F32, 0)
        h1_hi = at("h1_hi", [P, T], F32R, 4 * T)
        h1_lo = at("h1_lo", [P, T], F32R, 8 * T)
        h2 = at("h2", [P, T], F32, 12 * T)
        h2_hi = at("h2_hi", [P, T], F32R, 16 * T)
        h2_lo = at("h2_lo", [P, T], F32R, 20 * T)
        h3 = at("h3", [P, T], F32, 24 * T)

        ident = sb("ident", [P, P])
        ident16 = sb("ident16", [P, P], F16)
        ones = sb("ones", [D, P])
        w1_sb = sb("w1_sb", [D, H])
        b1_sb = sb("b1_sb", [1, H])
        ln_g_sb = sb("ln_g_sb", [1, H])
        ln_b_sb = sb("ln_b_sb", [H, 1])
        w2_sb = sb("w2_sb", [H, D])
        b2_sb = sb("b2_sb", [P, 1])
        wi_sb = sb("wi_sb", [P, H])
        wi_part = sb("wi_part", [P, 2, H], F32R)
        bi_sb = sb("bi_sb", [P, 1])
        wo_sb = sb("wo_sb", [H, D])
        bo_sb = sb("bo_sb", [P, 1])
        mask_sb = sb("mask_sb", [1, 2 * PARTS, ROWS])
        mask16 = sb("mask16", [1, 2 * PARTS, ROWS], BF16)
        shared_sb = sb("shared_sb", [P, 1, EROW])
        table = sb("table", [P, 2, E + 1, 2 * H], F32R)
        table_b = sb("table_b", [P, E + 1, 2])
        route_i = sb("route_i", [1, B * NG], I32)
        route_f = sb("route_f", [1, 3, B * NG])
        route_e = sb("route_e", [1, B * NG], I32)

        x_sb = sb("x_sb", [P, P], I32)
        fold = sb("fold", [P, 3, H])
        fold2 = sb("fold2", [P, 3, H])
        stat = sb("stat", [P, 12])
        tok_a = sb("tok_a", [P, 3, P])
        tok_v = sb("tok_v", [P, P])
        tok_y = sb("tok_y", [P, 4, P])
        mr = sb("mr", [P, 2, P])
        mr_rest = sb("mr_rest", [P, 2, 2, P])
        mr_part = sb("mr_part", [P, PARTS, 2, P], BF16)
        gw = sb("gw", [1, 2, H])
        gw_rest = sb("gw_rest", [1, 2, 2, H])
        gw_part = sb("gw_part", [1, PARTS, 2, H], BF16)
        mlp_w = sb("mlp_w", [ROWS, H], BF16)
        warm = sb("warm", [P, 2])
        h_t = sb("h_t", [P, 2, HALF])

        h_all = sb("h_all", [P, B * NT * D])

        probs = sb("probs", [P, 4, T])
        xn = sb("xn", [P, 2, NT * D])
        xc = sb("xc", [P, NT * D])
        xsq = sb("xsq", [P, NT * D])
        hl = sb("hl", [P, NT, 2 * D], F16)
        hi_lo = sb("hi_lo", [P, 2, T], F16)
        lo_hi = sb("lo_hi", [P, 2, T], F16)
        lnstat = sb("lnstat", [P, 2, 4, NT])
        minus_half = sb("minus_half", [P, NT])
        eps_sb = sb("eps_sb", [P, NT])
        denom = sb("denom", [P, 2, NT])
        rdenom = sb("rdenom", [P, NT])
        ctx_t = sb("ctx_t", [P, HALF])
        ctx_n = sb("ctx_n", [P, NT * D])
        h_mid = sb("h_mid", [P, 2, NT * D])

        yn = sb("yn", [P, NT * D])
        yc = sb("yc", [P, NT * D])
        ysq = sb("ysq", [P, NT * D])
        hl2 = sb("hl2", [P, NT, 2 * D], F16)
        hi_lo2 = sb("hi_lo2", [P, T], F32R)
        wsel_b = sb("wsel_b", [P, 2, NG, 2])
        y_t = sb("y_t", [P, HALF])
        y_out = sb("y_out", [P, 2, NT * D])

        ps_s = ctx.enter_context(nc.psum_tensor("ps_s", [P, 2, T], F32))
        ps_o = ctx.enter_context(nc.psum_tensor("ps_o", [P, HALF], F32))
        ps_a = ctx.enter_context(nc.psum_tensor("ps_a", [P, HALF], F32))
        ps_b = ctx.enter_context(nc.psum_tensor("ps_b", [P, HALF], F32))
        ps_c = ctx.enter_context(nc.psum_tensor("ps_c", [P, HALF], F32))

        staging = stage[:, :].rearrange("p (e r) -> p e r", r=EROW)
        scratch = nc.dram_tensor("mlp_rows", [2 * PARTS, B * T], BF16, kind="Internal").ap()

        s_load = {k: sem(f"s_load_{k}") for k in ("w1", "rows", "x", "w2", "ln_b", "route", "ffn", "table")}
        s_ident = sem("s_ident")
        s_ones = sem("s_ones")
        s_half = sem("s_half")
        s_warm = sem("s_warm")
        s_prep = sem("s_prep")
        s_usum = sem("s_usum")
        s_gw = sem("s_gw")
        s_gw_rows = sem("s_gw_rows")
        s_scratch = [sem(f"s_scratch{c}") for c in range(2)]
        s_rows = [sem(f"s_rows{c}") for c in range(2)]
        s_route = sem("s_route")
        s_wi = sem("s_wi")
        s_table = sem("s_table")
        s_hid = sem("s_hid")
        s_gelu = sem("s_gelu")
        s_w2 = sem("s_w2")
        s_ht = sem("s_ht")
        s_htt = sem("s_htt")
        s_h = sem("s_h")
        LN = ("sum", "cen", "sq", "ssq", "var", "rstd", "norm", "hi", "lo")
        n1 = {k: sem(f"s_n1_{k}") for k in LN}
        n2 = {k: sem(f"s_n2_{k}") for k in LN}
        s_xt = sem("s_xt")
        s_hilo = sem("s_hilo")
        s_swap = [sem(f"s_swap{i}") for i in range(2)]
        s_score = sem("s_score")
        s_exp = sem("s_exp")
        s_pv = sem("s_pv")
        s_ctx = sem("s_ctx")
        s_ctxt = sem("s_ctxt")
        s_rden = sem("s_rden")
        s_ctxn = sem("s_ctxn")
        s_res = sem("s_res")
        s_yt = sem("s_yt")
        s_hilo2 = sem("s_hilo2")
        s_in = sem("s_in")
        s_h1 = sem("s_h1")
        s_h1_hi = sem("s_h1_hi")
        s_h1_lo = sem("s_h1_lo")
        s_l1 = sem("s_l1")
        s_h2 = sem("s_h2")
        s_h2_hi = sem("s_h2_hi")
        s_h2_lo = sem("s_h2_lo")
        s_l2 = sem("s_l2")
        s_h3 = sem("s_h3")
        s_wo = sem("s_wo")
        s_y = sem("s_y")
        s_ytt = sem("s_ytt")
        s_out = sem("s_out")
        s_sel = [sem(f"s_sel{i}") for i in range(2)]
        s_store = [sem(f"s_store{i}") for i in range(2)]

        block = ctx.enter_context(nc.Block())

        def wait(eng, s, n):
            if not isinstance(n, int) or n > 0:
                eng.wait_ge(s, n)

        def pipeline(eng, turn, first, last):
            def whole(i):
                turn(i, i % 2, lambda d: 0 <= i + d < B)
            for i in range(first):
                whole(i)
            with eng.Fori(0, (last + 1 - first) // 2) as pair:
                turn(pair * 2 + first, first % 2, lambda d: True)
                turn(pair * 2 + (first + 1), (first + 1) % 2, lambda d: True)
            for i in range(last + 1, B + 2):
                whole(i)

        MLP_LOOP = (7, B - 4)
        CENTRE_TURN = (3, B - 2)
        SQUARE_TURN = (4, B - 1)
        NORM_TURN, X_TURN = 6, B - 3
        MAIN_LOOP = (4, B - 3)
        CHUNKS = ((0, 2 * T), (2 * T, B * T))

        def last(i):
            return isinstance(i, int) and i == B

        def tiles(ap):
            return ap.rearrange("p (k d) -> p k d", d=D)

        def halves(ap):
            return ap.rearrange("p (j f d) -> p f j d", f=2, d=D)

        def by_half(ap):
            return ap.rearrange("p (f j d) -> p f j d", f=2, d=D)

        def over_d(ap):
            return ap.unsqueeze(2).to_broadcast([P, NT, D])

        def batch(ap, i, n=NT * D):
            return ap[:, bass.ts(i, n)]

        @block.sync
        def _(sp):
            sp.dma_start(w1_sb[:, :], w1).then_inc(s_load["w1"], 16)
            sp.dma_start(b1_sb[:, :], b1).then_inc(s_load["w1"], 16)
            sp.dma_start(mask_sb[:, :, :], row_mask).then_inc(s_load["rows"], 16)
            sp.dma_start(w2_sb[:, :], w2).then_inc(s_load["w2"], 16)
            sp.dma_start(b2_sb[:, :], b2x2).then_inc(s_load["w2"], 16)
            sp.wait_ge(s_prep, PREP_PARTS)
            for c, (a, z) in enumerate(CHUNKS):
                sp.dma_start(scratch[:, a:z].rearrange("(n k) (p f) -> p n k f", k=2, f=P),
                             mr_part[a // P:z // P, :, :, :]).then_inc(s_scratch[c], 16)
            for c, (a, z) in enumerate(CHUNKS):
                sp.wait_ge(s_scratch[c], 16)
                sp.dma_start(mlp_x[:, a:z], scratch[:, a:z].unsqueeze(0).to_broadcast([PARTS, 2 * PARTS, z - a]))\
                  .then_inc(s_rows[c], 16)

            def swap(b, q):
                wait(sp, s_hilo, b + 1)
                wait(sp, s_score, 8 * (b - 1))
                sp.dma_start(lo_hi[0:D, q, :], hi_lo[D:P, q, :]).then_inc(s_swap[q], 16)
                sp.dma_start(lo_hi[D:P, q, :], hi_lo[0:D, q, :]).then_inc(s_swap[q], 16)

            swap(0, 0)
            sp.wait_ge(s_route, 5)
            sp.wait_ge(s_table, TABLE_STEPS)

            def turn(i, q, has):
                if has(-1):
                    b = i - 1
                    wait(sp, s_h3, 4 * (b - 1))
                    for g in range(NG):
                        e = sp.value_load(route_e[0:1, bass.ds(b * NG + g, 1)], min_val=0, max_val=E)
                        sp.dma_start(wsel[:, 1 - q, g, :, :].bitcast(F32), table[:, :, bass.ds(e, 1), :].bitcast(F32))\
                          .then_inc(s_sel[1 - q], 16)
                        sp.dma_start(wsel_b[:, 1 - q, g, :], table_b[:, bass.ds(e, 1), :]).then_inc(s_sel[1 - q], 16)
                if has(1):
                    swap(i + 1, 1 - q)
                if has(-2):
                    b = i - 2
                    wait(sp, s_out, b + 1)
                    sp.dma_start(out[bass.ds(b, 1), :, :].rearrange("o (k p) d -> p (o k) d", p=P),
                                 tiles(y_out[:, q, :])).then_inc(s_store[q], 16)

            pipeline(sp, turn, *MAIN_LOOP)
            for q in range(2):
                sp.wait_ge(s_store[q], 16 * B // 2)

        @block.gpsimd
        def _(pool):
            pool.memset(ident[:, :], 0.0).then_inc(s_ident, 1)
            pool.memset(ident16[:, :], 0.0).then_inc(s_ident, 1)
            pool.wait_ge(s_ident, 2)
            for m in (ident, ident16):
                pool.affine_select(out=m[:, :], in_=m[:, :], compare_op=ALU.not_equal, fill=1.0, base=0,
                                   pattern=[[-1, P]], channel_multiplier=1).then_inc(s_ident, 1)
            pool.memset(minus_half[:, :], -0.5).then_inc(s_half, 1)
            pool.memset(eps_sb[:, :], EPS).then_inc(s_half, 1)
            steps = [0]

            def step(ins):
                steps[0] += 1
                ins.then_inc(s_gw, 1)
                pool.wait_ge(s_gw, steps[0])

            pool.wait_ge(s_load["rows"], 32)
            pool.dma_start(staging, experts).then_inc(s_load["table"], 16)
            pool.dma_start(shared_sb[:, 0, :], shared).then_inc(s_load["table"], 16)
            step(pool.tensor_copy(mask16[:, :, :], mask_sb[:, :, :]))
            pool.wait_ge(s_prep, PREP_FOLD)
            for n in range(2):
                step(pool.tensor_tensor(gw[:, n, :], fold[0:1, n, :], ln_g_sb[:, :], ALU.mult))
            src = gw[:, :, :]
            for n in range(PARTS):
                step(pool.tensor_copy(gw_part[:, n], src))
                if n < PARTS - 1:
                    step(pool.tensor_tensor(gw_rest[:, n], src, gw_part[:, n], ALU.subtract))
                    src = gw_rest[:, n]
            assert steps[0] == GW_STEPS

            pool.wait_ge(s_load["table"], 32)
            pool.wait_ge(s_ident, 4)
            made = [0]

            def entry(ins, chained=True):
                made[0] += 1
                ins.then_inc(s_table, 1)
                if chained:
                    pool.wait_ge(s_table, made[0])

            for n in range(2):
                m = shared_sb[:, 0, n * H:(n + 1) * H]
                entry(pool.tensor_tensor(m, m, ident[:, :], ALU.add))
            w = shared_sb[:, :, 0:2 * H]
            entry(pool.tensor_copy(table[:, 0, E:E + 1, :], w))
            entry(pool.tensor_tensor(table[:, 1, E:E + 1, :], w, table[:, 0, E:E + 1, :].bitcast(F32), ALU.subtract))
            entry(pool.tensor_copy(table_b[:, E:E + 1, :], shared_sb[:, :, 2 * H:]))

            def experts_to_table(n):
                m, hi = staging[:, n:n + CHUNK, :], table[:, 0, n:n + CHUNK, :]
                added = shared_sb[:, :, :].to_broadcast([P, CHUNK, EROW])
                entry(pool.tensor_tensor(hi, m[:, :, 0:2 * H], added[:, :, 0:2 * H], ALU.add))
                entry(pool.tensor_tensor(m, m, added, ALU.add))
                entry(pool.tensor_tensor(table[:, 1, n:n + CHUNK, :], m[:, :, 0:2 * H], hi.bitcast(F32), ALU.subtract),
                      chained=False)
                entry(pool.tensor_copy(table_b[:, n:n + CHUNK, :], m[:, :, 2 * H:]))

            def rstd(n, s, b):
                wait(pool, s["ssq"], b + 1)
                wait(pool, s["norm"], b)
                pool.tensor_tensor(lnstat[:, n, 2, :], lnstat[:, n, 1, :], eps_sb[:, :], ALU.add)\
                    .then_inc(s["var"], 1)
                wait(pool, s["var"], b + 1)
                pool.tensor_tensor(lnstat[:, n, 3, :], lnstat[:, n, 2, :], minus_half[:, :], ALU.pow)\
                    .then_inc(s["rstd"], 1)

            def low(s, x_n, x_hl, b):
                wait(pool, s["hi"], b + 1)
                pool.tensor_tensor(x_hl[:, :, D:2 * D], tiles(x_n), x_hl[:, :, 0:D], ALU.subtract)\
                    .then_inc(s["lo"], 1)

            pool.wait_ge(s_half, 2)
            for n in range(0, E, CHUNK):
                if n == 2 * CHUNK:
                    rstd(0, n1, 0)
                    low(n1, xn[:, 0, :], hl, 0)
                experts_to_table(n)
            rstd(0, n1, 1)
            assert made[0] == TABLE_STEPS, made[0]

            def turn(i, q, has):
                if has(1):
                    low(n1, xn[:, 1 - q, :], hl, i + 1)
                if has(-1):
                    rstd(1, n2, i - 1)
                    if not last(i):
                        low(n2, yn[:, :], hl2, i - 1)
                if has(2):
                    rstd(0, n1, i + 2)

            pipeline(pool, turn, *MAIN_LOOP)

        @block.tensor
        def _(pe):
            def keep_awake(n, bank):
                for _ in range(n):
                    pe.matmul(bank, ident16[:, :], ident16[:, :].unsqueeze(1).to_broadcast([P, HALF // P, P]),
                              start=True, stop=True)

            pe.wait_ge(s_load["w1"], 32)
            pe.wait_ge(s_ones, 1)
            pe.matmul(ps_a[:, 0:H], ones[:, :], w1_sb[:, :], start=True, stop=True).then_inc(s_usum, 1)
            pe.matmul(ps_a[:, H:2 * H], ones[0:1, :], b1_sb[:, :], start=True, stop=True).then_inc(s_usum, 1)
            pe.wait_ge(s_gw, GW_STEPS)
            for v in range(2):
                for n in range(PARTS):
                    t = PARTS * v + n
                    m = pe.matmul(ps_b[0:ROWS, 0:H], mask16[:, t, :], gw_part[:, n, v, :],
                                  start=(t == 0), stop=(t == 2 * PARTS - 1))
            m.then_inc(s_gw_rows, 1)
            keep_awake(20, ps_c[:, :])
            pe.wait_ge(s_gw_rows, 2)
            pe.wait_ge(s_ident, 4)
            pe.wait_ge(s_load["w2"], 32)
            hid = (ps_o, ps_a)
            tps = (ps_b, ps_c)

            def x_transposes(b, bank):
                wait(pe, n1["lo"], b + 1)
                for k in range(NT):
                    m = pe.transpose(bank.bitcast(F16)[:, k * P:(k + 1) * P], hl[:, k, :], ident16[:, :])
                m.then_inc(s_xt, 1)

            def scores(i, q, g):
                if g == 0:
                    wait(pe, s_hilo, i + 1)
                    pe.wait_ge(s_swap[q], (i - q) * 16 + 32)
                for c in (2 * g, 2 * g + 1):
                    wait(pe, s_exp, 8 * i + c - 1)
                    for f in range(2):
                        o = ps_s[:, c % 2, f * HALF:(f + 1) * HALF]
                        k = hi_lo[:, q, c * P:(c + 1) * P]
                        pe.matmul(o, k, hi_lo[:, q, f * HALF:(f + 1) * HALF], start=True, stop=False)
                        m = pe.matmul(o, k, lo_hi[:, q, f * HALF:(f + 1) * HALF], start=False, stop=True)
                    m.then_inc(s_score, 1)

            def mlp_turn(i, q, has):
                if isinstance(i, int) and i == B + 1:
                    scores(0, 0, 0)
                if has(0):
                    for c in range(2):
                        if isinstance(i, int) and i == CHUNKS[c][0] // T:
                            pe.wait_ge(s_rows[c], 16)
                    wait(pe, s_gelu, i - 1)
                    for f in range(2):
                        m = pe.matmul(ps_s[:, q, f * HALF:(f + 1) * HALF], mlp_w[:, :],
                                      mlp_x[:, bass.ds(i * T + f * HALF, HALF)], start=True, stop=True)
                    m.then_inc(s_hid, 1)
                if has(-1):
                    b = i - 1
                    wait(pe, s_gelu, b + 1)
                    wait(pe, s_ht, b - 1)
                    for f in range(2):
                        m = pe.matmul(hid[1 - q][f * D:(f + 1) * D, :], w2_sb[:, :],
                                      probs[:, 1 - q, f * HALF:(f + 1) * HALF], start=True, stop=True)
                    m.then_inc(s_w2, 1)
                if has(-2):
                    b = i - 2
                    wait(pe, s_ht, b + 1)
                    wait(pe, s_h, b - 1)
                    if isinstance(i, int) and i == X_TURN + 1:
                        pe.wait_ge(s_hilo, 1)
                    for j in range(NT // 2):
                        m = pe.transpose(tps[q][:, j * P:(j + 1) * P], h_t[:, q, j * P:(j + 1) * P], ident[:, :])
                    m.then_inc(s_htt, 1)
                if isinstance(i, int) and i == X_TURN:
                    wait(pe, s_h, i - 2)
                    x_transposes(0, tps[1 - q][:, :])

            pipeline(pe, mlp_turn, *MLP_LOOP)

            def context(i, q, g):
                if g == 0:
                    wait(pe, s_ctx, i)
                for c in (2 * g, 2 * g + 1):
                    wait(pe, s_exp, 8 * i + c + 1)
                    for f in range(2):
                        m = pe.matmul(ps_o[f * D:(f + 1) * D, :], xn[:, q, c * D:(c + 1) * D],
                                      probs[:, c % 4, f * HALF:(f + 1) * HALF], start=(c == 0), stop=(c == NT - 1))
                    m.then_inc(s_pv, 1)

            def layer(b, q, n, hi_there, lo_there, x_hi, x_lo, done):
                for f, bank in enumerate((ps_a, ps_b)):
                    wait(pe, hi_there, NG * b + 2 * f + 2)
                    for g in (2 * f, 2 * f + 1):
                        o = bank[:, (g % 2) * GROUP:(g % 2 + 1) * GROUP]
                        hi, lo = (x[:, g * GROUP:(g + 1) * GROUP] for x in (x_hi, x_lo))
                        w_hi, w_lo = (wsel[:, q, g, t, n * H:(n + 1) * H] for t in range(2))
                        pe.matmul(o, w_hi, hi, start=True, stop=False)
                        pe.matmul(o, w_lo, hi, start=False, stop=False)
                        wait(pe, lo_there, NG * b + g + 1)
                        m = pe.matmul(o, w_hi, lo, start=False, stop=True)
                    m.then_inc(done, 1)

            def y_transposes(b, bank):
                wait(pe, s_y, b + 1)
                for j in range(NT // 2):
                    m = pe.transpose(bank[:, j * P:(j + 1) * P], y_t[:, j * P:(j + 1) * P], ident[:, :])
                m.then_inc(s_ytt, 1)

            def turn(i, q, has):
                b = i - 2
                if has(0) and not (isinstance(i, int) and i == 0):
                    scores(i, q, 0)
                if has(-1):
                    context(i - 1, 1 - q, 3)
                if has(-2):
                    wait(pe, s_sel[q], (b - q) * 64 + 128)
                    layer(b, q, 0, s_h1_hi, s_h1_lo, h1_hi, h1_lo, s_l1)
                if has(-1):
                    wait(pe, s_ctx, i)
                    for j in range(NT // 2):
                        m = pe.transpose(ps_c[:, j * P:(j + 1) * P], ctx_t[:, j * P:(j + 1) * P], ident[:, :])
                    m.then_inc(s_ctxt, 1)
                if has(0):
                    scores(i, q, 1)
                if last(i):
                    keep_awake(18, ps_s[:, 1, 0:HALF])
                if has(-2):
                    layer(b, q, 1, s_h2_hi, s_h2_lo, h2_hi, h2_lo, s_l2)
                if has(0):
                    context(i, q, 0)
                if has(-2):
                    for f in range(2):
                        wait(pe, s_h3, 4 * b + 2 * f + 2)
                        m = pe.matmul(ps_a[f * D:(f + 1) * D, :], wo_sb[:, :], h3[:, f * HALF:(f + 1) * HALF],
                                      start=True, stop=True)
                    m.then_inc(s_wo, 1)
                if has(0):
                    scores(i, q, 2)
                if has(1):
                    wait(pe, s_ctxn, i)
                    x_transposes(i + 1, ps_c[:, :])
                if has(-2) and not last(i):
                    y_transposes(b, ps_b)
                if has(0):
                    context(i, q, 1)
                if has(0):
                    scores(i, q, 3)
                if has(-1):
                    c = i - 1
                    bank = (ps_s[:, 0, 0:HALF] if last(i) else ps_a[:, :]).bitcast(F16)
                    wait(pe, n2["lo"], c + 1)
                    for k in range(NT):
                        m = pe.transpose(bank[:, k * P:(k + 1) * P], hl2[:, k, :], ident16[:, :])
                    m.then_inc(s_yt, 1)
                if has(0):
                    context(i, q, 2)
                if last(i):
                    y_transposes(b, ps_o)
                if has(-1):
                    wait(pe, s_out, c - 1 if last(i) else c)
                    wait(pe, s_hilo, min(i + 2, B) if isinstance(i, int) else i + 2)
                    if isinstance(i, int) and i == 1:
                        pe.wait_ge(s_wi, 2)
                        pe.wait_ge(s_load["ffn"], 16 * 5)
                    for f, bank in enumerate((ps_b, ps_c)):
                        wait(pe, s_hilo2, 2 * c + f + 1)
                        for n in range(2):
                            m = pe.matmul(bank[:, :], wi_part[:, n, :], hi_lo2[:, f * HALF:(f + 1) * HALF],
                                          start=(n == 0), stop=(n == 1))
                        m.then_inc(s_in, 1)

            pipeline(pe, turn, *MAIN_LOOP)

        @block.scalar
        def _(act):
            act.dma_start(x_sb[:, :], x.rearrange("b (q f) -> (b q) f", f=P)).then_inc(s_load["x"], 16)
            act.dma_start(ln_g_sb[:, :], ln_g).then_inc(s_load["rows"], 16)
            act.dma_start(ln_b_sb[:, :], ln_b_col).then_inc(s_load["ln_b"], 16)
            act.dma_start(route_i[:, :], route).then_inc(s_load["route"], 16)
            act.dma_start(wi_sb[0:D, :], wi_t).then_inc(s_load["ffn"], 16)
            act.dma_start(wi_sb[D:P, :], wi_t).then_inc(s_load["ffn"], 16)
            act.dma_start(bi_sb[:, :], bi).then_inc(s_load["ffn"], 16)
            act.dma_start(wo_sb[:, :], wo_t).then_inc(s_load["ffn"], 16)
            act.dma_start(bo_sb[:, :], box2).then_inc(s_load["ffn"], 16)
            act.wait_ge(s_half, 2)
            act.activation(warm[:, 0:1], eps_sb[:, 0:1], ACT.Gelu).then_inc(s_warm, 1)
            act.wait_ge(s_gw_rows, 1)
            act.activation(mlp_w[:, :], ps_b[0:ROWS, 0:H], ACT.Identity).then_inc(s_gw_rows, 1)
            act.wait_ge(s_load["ln_b"], 16)

            def mlp_turn(i, q, has):
                if has(0):
                    wait(act, s_hid, i + 1)
                    wait(act, s_w2, i - 1)
                    act.activation(probs[:, q, :], ps_s[:, q, :], ACT.Gelu, bias=ln_b_sb[:, :]).then_inc(s_gelu, 1)
                for b in range(2):
                    if isinstance(i, int) and i == SQUARE_TURN[b]:
                        square(n1, xsq, xc, b)

            def square(s, dst, src, b):
                wait(act, s["cen"], b + 1)
                wait(act, s["ssq"], b)
                act.activation(dst[:, :], src[:, :], ACT.Square, scale=float(D) ** -0.5).then_inc(s["sq"], 1)

            pipeline(act, mlp_turn, *MLP_LOOP)
            act.activation(warm[:, 1:2], eps_sb[:, 0:1], ACT.Exp).then_inc(s_warm, 1)
            act.wait_ge(s_w2, B)

            def exps(i, q, g):
                for c in (2 * g, 2 * g + 1):
                    if c == 0:
                        wait(act, s_rden, i - 1)
                    wait(act, s_score, 8 * i + c + 1)
                    wait(act, s_pv, 8 * i + c - 3)
                    act.activation(probs[:, c % 4, :], ps_s[:, c % 2, :], ACT.Exp, scale=float(D) ** -0.5,
                                   accum_out=denom[:, q, c:c + 1]).then_inc(s_exp, 1)

            def relus(i, q, n, dst, src_done, read, per, done):
                b = i - 2
                for g in range(NG):
                    if g % 2 == 0:
                        wait(act, src_done, 2 * b + g // 2 + 1)
                    if g == 0:
                        wait(act, read, per * b)
                        wait(act, s_sel[q], (b - q) * 64 + 128)
                    bank = (ps_a, ps_b)[g // 2]
                    act.activation(dst[:, g * GROUP:(g + 1) * GROUP], bank[:, (g % 2) * GROUP:(g % 2 + 1) * GROUP],
                                   ACT.Relu, bias=wsel_b[:, q, g, n:n + 1]).then_inc(done, 1)

            def turn(i, q, has):
                if has(0):
                    exps(i, q, 0)
                if has(-2):
                    relus(i, q, 0, h2, s_l1, s_h2_lo, NG, s_h2)
                if has(0):
                    exps(i, q, 1)
                if last(i):
                    square(n2, ysq, yc, i - 1)
                if has(-2):
                    relus(i, q, 1, h3, s_l2, s_wo, 1, s_h3)
                if has(-1) and not last(i):
                    square(n2, ysq, yc, i - 1)
                if last(i):
                    act.wait_ge(s_wo, i - 1)
                    act.wait_ge(s_ytt, i - 2)
                    act.activation(y_t[:, :], ps_a[:, :], ACT.Identity, bias=bo_sb[:, :]).then_inc(s_y, 1)
                if has(0):
                    exps(i, q, 2)
                if has(2):
                    square(n1, xsq, xc, i + 2)
                if has(0):
                    exps(i, q, 3)
                if has(-1):
                    b = i - 1
                    for f, bank in enumerate((ps_b, ps_c)):
                        wait(act, s_in, 2 * b + f + 1)
                        wait(act, s_h1_lo, NG * b)
                        act.activation(h1[:, f * HALF:(f + 1) * HALF], bank[:, :], ACT.Relu, bias=bi_sb[:, :])\
                           .then_inc(s_h1, 1)

            pipeline(act, turn, *MAIN_LOOP)

        @block.vector
        def _(dve):
            done = [0]

            def step(ins, chained=True):
                done[0] += 1
                ins.then_inc(s_prep, 1)
                if chained:
                    dve.wait_ge(s_prep, done[0])

            dve.memset(ones[:, :], 1.0).then_inc(s_ones, 1)
            dve.wait_ge(s_load["x"], 16)
            step(dve.tensor_scalar(tok_a[:, 0, :], x_sb[:, :], 1.0 / 127.5, -1.0, ALU.mult, ALU.add))
            step(dve.tensor_scalar(tok_a[:, 1, :], tok_a[:, 0, :], -1.0, None, ALU.mult))
            step(dve.tensor_tensor(tok_a[:, 2, :], tok_a[:, 0, :], tok_a[:, 1, :], ALU.max))
            dve.wait_ge(s_usum, 2)
            rows = ps_a[:, 0:2 * H].rearrange("p (v h) -> p v h", h=H)
            step(dve.tensor_reduce(stat[:, 0:2], rows, AX.X, ALU.add))
            step(dve.scalar_tensor_tensor(fold[:, 0:2, :], stat[:, 0:2].unsqueeze(2).to_broadcast([P, 2, H]), -1.0 / H,
                                          rows, ALU.mult, ALU.add))
            assert done[0] == PREP_FOLD, done[0]
            step(dve.tensor_tensor(fold2[:, 0:2, :], fold[:, 0:2, :], fold[:, 0:1, :].to_broadcast([P, 2, H]),
                                   ALU.mult))
            step(dve.tensor_reduce(stat[:, 4:6], fold2[:, 0:2, :], AX.X, ALU.add))
            step(dve.tensor_scalar(stat[:, 6:7], stat[:, 4:5], TINY, None, ALU.max))
            step(dve.reciprocal(stat[:, 7:8], stat[:, 6:7]))
            step(dve.tensor_tensor(stat[:, 8:9], stat[:, 5:6], stat[:, 7:8], ALU.mult))
            step(dve.tensor_scalar(tok_y[:, 0, :], tok_a[:, 2, :], stat[:, 8:9], None, ALU.add), chained=False)
            step(dve.tensor_scalar(stat[:, 2:3], stat[:, 4:5], 1.0 / H, None, ALU.mult), chained=False)
            step(dve.scalar_tensor_tensor(fold[:, 2, :], fold[:, 0, :], stat[:, 8:9], fold[:, 1, :],
                                          ALU.mult, ALU.subtract))
            step(dve.tensor_tensor(fold2[:, 2, :], fold[:, 2, :], fold[:, 2, :], ALU.mult), chained=False)
            step(dve.scalar_tensor_tensor(tok_y[:, 1, :], tok_y[:, 0, :], stat[:, 2:3], tok_y[:, 0, :],
                                          ALU.mult, ALU.mult))
            step(dve.tensor_reduce(stat[:, 9:10], fold2[:, 2, :], AX.X, ALU.add))
            step(dve.tensor_scalar(stat[:, 10:11], stat[:, 9:10], 1.0 / H, EPS, ALU.mult, ALU.add))
            step(dve.tensor_scalar(tok_v[:, :], tok_y[:, 1, :], stat[:, 10:11], None, ALU.add))
            step(dve.tensor_scalar(tok_y[:, 0, :].bitcast(I32), tok_v[:, :].bitcast(I32), -0.5, RSQRT_SEED,
                                   ALU.mult, ALU.add))
            for n in range(3):
                y, y_next = tok_y[:, n % 2, :], (tok_y[:, (n + 1) % 2, :] if n < 2 else mr[:, 1, :])
                step(dve.scalar_tensor_tensor(tok_y[:, 2, :], y, -0.5, y, ALU.mult, ALU.mult))
                step(dve.tensor_tensor(tok_y[:, 3, :], tok_y[:, 2, :], tok_v[:, :], ALU.mult))
                step(dve.scalar_tensor_tensor(y_next, tok_y[:, 3, :], 1.5, y, ALU.add, ALU.mult))
            step(dve.tensor_tensor(mr[:, 0, :], tok_a[:, 2, :], mr[:, 1, :], ALU.mult))

            def split(parts, whole, rest):
                src = whole
                for n in range(PARTS):
                    step(dve.tensor_copy(parts[n], src))
                    if n < PARTS - 1:
                        step(dve.tensor_tensor(rest[n], src, parts[n], ALU.subtract))
                        src = rest[n]

            split([mr_part[:, n] for n in range(PARTS)], mr[:, :, :], [mr_rest[:, n] for n in range(2)])
            assert done[0] == PREP_PARTS, done[0]
            dve.wait_ge(s_load["route"], 16)
            dve.tensor_scalar(route_f[:, 0, :], route_i[:, :], -float(E), None, ALU.add).then_inc(s_route, 1)
            dve.tensor_scalar(route_f[:, 1, :], route_i[:, :], 0.0, None, ALU.is_ge).then_inc(s_route, 1)
            dve.wait_ge(s_route, 2)
            dve.scalar_tensor_tensor(route_f[:, 2, :], route_i[:, :], float(E - 1), route_f[:, 1, :],
                                     ALU.is_le, ALU.mult).then_inc(s_route, 1)
            dve.wait_ge(s_route, 3)
            dve.tensor_tensor(route_f[:, 1, :], route_f[:, 0, :], route_f[:, 2, :], ALU.mult).then_inc(s_route, 1)
            dve.wait_ge(s_route, 4)
            dve.tensor_scalar(route_e[:, :], route_f[:, 1, :], float(E), None, ALU.add).then_inc(s_route, 1)
            dve.wait_ge(s_load["ffn"], 16 * 5)
            dve.tensor_copy(wi_part[:, 0, :], wi_sb[:, :]).then_inc(s_wi, 1)
            dve.wait_ge(s_wi, 1)
            dve.tensor_tensor(wi_part[:, 1, :], wi_sb[:, :], wi_part[:, 0, :].bitcast(F32), ALU.subtract)\
               .then_inc(s_wi, 1)

            hid = (ps_o, ps_a)
            tps = (ps_b, ps_c)

            def mlp_turn(i, q, has):
                if has(-1):
                    b = i - 1
                    wait(dve, s_w2, b + 1)
                    wait(dve, s_htt, b - 1)
                    dve.tensor_scalar(h_t[:, 1 - q, :], hid[1 - q][:, :], b2_sb[:, :], None, ALU.add)\
                       .then_inc(s_ht, 1)
                if has(-2):
                    b = i - 2
                    wait(dve, s_htt, b + 1)
                    dve.tensor_copy(by_half(batch(h_all, b)), halves(tps[q][:, :])).then_inc(s_h, 1)
                for b in range(2):
                    if isinstance(i, int) and i == CENTRE_TURN[b]:
                        dve.wait_ge(s_h, b + 1)
                        wait(dve, n1["norm"], b)
                        centre(0, n1, b, batch(h_all, b), xc)
                    if isinstance(i, int) and i == SQUARE_TURN[b]:
                        squares(0, n1, b, xsq)
                if isinstance(i, int) and i == NORM_TURN:
                    norm(0, n1, 0, xc, xn[:, 0, :], hl)
                if isinstance(i, int) and i == X_TURN:
                    x_out(0, 0, tps[1 - q][:, :])

            def centre(n, s, b, x, x_c):
                dve.tensor_reduce(lnstat[:, n, 0, :], tiles(x), AX.X, ALU.add).then_inc(s["sum"], 1)
                wait(dve, s["sum"], b + 1)
                dve.scalar_tensor_tensor(tiles(x_c[:, :]), over_d(lnstat[:, n, 0, :]), -1.0 / D,
                                         tiles(x), ALU.mult, ALU.add).then_inc(s["cen"], 1)

            def squares(n, s, b, x_sq):
                wait(dve, s["sq"], b + 1)
                wait(dve, s["var"], b)
                dve.tensor_reduce(lnstat[:, n, 1, :], tiles(x_sq[:, :]), AX.X, ALU.add).then_inc(s["ssq"], 1)

            def norm(n, s, b, x_c, x_n, x_hl):
                wait(dve, s["rstd"], b + 1)
                dve.tensor_tensor(tiles(x_n), tiles(x_c[:, :]), over_d(lnstat[:, n, 3, :]), ALU.mult)\
                   .then_inc(s["norm"], 1)
                wait(dve, s["norm"], b + 1)
                dve.tensor_copy(x_hl[:, :, 0:D], tiles(x_n)).then_inc(s["hi"], 1)

            def x_out(b, q, bank):
                wait(dve, s_xt, b + 1)
                wait(dve, s_score, 8 * (b - 1))
                if not isinstance(b, int) or b >= 2:
                    dve.wait_ge(s_swap[q], (b - q) * 16)
                dve.tensor_copy(hi_lo[:, q, :], bank.bitcast(F16)).then_inc(s_hilo, 1)

            dve.wait_ge(s_load["w2"], 32)
            pipeline(dve, mlp_turn, *MLP_LOOP)
            dve.wait_ge(s_h, B)

            def parts(b, f, src, hi, lo, there, per, read, hi_done, lo_done):
                groups = [(g, slice(g * GROUP, (g + 1) * GROUP)) for g in (2 * f, 2 * f + 1)]
                wait(dve, read, 2 * b)
                for g, h in groups:
                    wait(dve, there, per * b + g * per // NG + 1)
                    dve.tensor_copy(hi[:, h], src[:, h]).then_inc(hi_done, 1)
                for g, h in groups:
                    wait(dve, hi_done, NG * b + g + 1)
                    dve.tensor_tensor(lo[:, h], src[:, h], hi[:, h].bitcast(F32), ALU.subtract).then_inc(lo_done, 1)

            def result(b, q, bank):
                wait(dve, s_ytt, b + 1)
                if not isinstance(b, int) or b >= 2:
                    dve.wait_ge(s_store[q], (b - q) * 8)
                dve.tensor_tensor(by_half(y_out[:, q, :]), halves(bank[:, :]), by_half(h_mid[:, q, :]), ALU.add)\
                   .then_inc(s_out, 1)

            def turn(i, q, has):
                b = i - 1

                def h2_parts(f):
                    parts(i - 2, f, h2, h2_hi, h2_lo, s_h2, 4, s_l2, s_h2_hi, s_h2_lo)

                if has(-1):
                    wait(dve, s_pv, 8 * (b + 1))
                    wait(dve, s_ctxt, b)
                    dve.tensor_copy(ctx_t[:, :], ps_o[:, :]).then_inc(s_ctx, 1)
                if has(1):
                    wait(dve, s_xt, i + 1)
                    norm(0, n1, i + 1, xc, xn[:, 1 - q, :], hl)
                if has(-2) and not last(i):
                    h2_parts(0)
                    h2_parts(1)
                if has(-1):
                    wait(dve, s_exp, 8 * (b + 1))
                    dve.reciprocal(rdenom[:, :], denom[:, 1 - q, :]).then_inc(s_rden, 1)
                    wait(dve, s_rden, b + 1)
                    wait(dve, s_ctxt, b + 1)
                    rd = rdenom[:, :].rearrange("p (f j) -> p f j", f=2).unsqueeze(3).to_broadcast([P, 2, NT // 2, D])
                    dve.tensor_tensor(by_half(ctx_n[:, :]), halves(ps_c[:, :]), rd, ALU.mult).then_inc(s_ctxn, 1)
                    wait(dve, s_ctxn, b + 1)
                    dve.tensor_tensor(h_mid[:, 1 - q, :], batch(h_all, b), ctx_n[:, :], ALU.add).then_inc(s_res, 1)
                    wait(dve, s_res, b + 1)
                    centre(1, n2, b, h_mid[:, 1 - q, :], yc)
                if last(i):
                    h2_parts(0)
                if has(-1):
                    squares(1, n2, b, ysq)
                if last(i):
                    h2_parts(1)
                if has(-2) and not last(i):
                    wait(dve, s_wo, i - 1)
                    wait(dve, s_ytt, i - 2)
                    dve.tensor_scalar(y_t[:, :], ps_a[:, :], bo_sb[:, :], None, ALU.add).then_inc(s_y, 1)
                if has(2):
                    wait(dve, n1["norm"], i + 2)
                    centre(0, n1, i + 2, batch(h_all, i + 2), xc)
                if has(1):
                    x_out(i + 1, 1 - q, ps_c[:, :])
                if has(-1):
                    norm(1, n2, b, yc, yn[:, :], hl2)
                if last(i):
                    wait(dve, n2["hi"], b + 1)
                    dve.tensor_tensor(hl2[:, :, D:2 * D], tiles(yn[:, :]), hl2[:, :, 0:D], ALU.subtract)\
                       .then_inc(n2["lo"], 1)
                if has(2):
                    squares(0, n1, i + 2, xsq)
                if has(-2) and not last(i):
                    result(i - 2, q, ps_b)
                if has(-1):
                    wait(dve, s_yt, b + 1)
                    wait(dve, s_in, 2 * b)
                    bank = (ps_s[:, 0, 0:HALF] if last(i) else ps_a[:, :]).bitcast(F16)
                    for f in range(2):
                        h = slice(f * HALF, (f + 1) * HALF)
                        dve.tensor_copy(hi_lo2[:, h], bank[:, h]).then_inc(s_hilo2, 1)
                    if last(i):
                        result(i - 2, q, ps_o)
                    for f in range(2):
                        parts(b, f, h1, h1_hi, h1_lo, s_h1, 2, s_l1, s_h1_hi, s_h1_lo)

            pipeline(dve, turn, *MAIN_LOOP)


def kernel(x, L0_tok_W1, L0_tok_b1, L0_tok_ln_g, L0_tok_ln_b, L0_tok_W2, L0_tok_b2, L0_ffn_route_id,
           L0_ffn_Wi, L0_ffn_bi, L0_ffn_Wr, L0_ffn_br, L0_ffn_Ws, L0_ffn_bs, L0_ffn_Wo, L0_ffn_bo):
    import numpy as np
    import concourse.bacc as bacc
    from concourse.bass_utils import run_bass_kernel_spmd

    def col(v):
        return np.asarray(v).reshape(-1, 1)

    row_mask = np.zeros((ROWS, 2 * PARTS), np.float32)
    for r in range(ROWS):
        row_mask[r, PARTS * (r % 2) + r // (2 * PARTS)] = 1.0
    wr = np.transpose(np.asarray(L0_ffn_Wr), (3, 1, 0, 2)).reshape(H, E, 2 * H)
    br = np.transpose(np.asarray(L0_ffn_br), (2, 1, 0))
    ws = np.transpose(np.asarray(L0_ffn_Ws)[:, 0], (2, 0, 1)).reshape(H, 2 * H)
    bs = np.transpose(np.asarray(L0_ffn_bs)[:, 0], (1, 0))
    arrays = {
        "x": np.asarray(x),
        "w1": np.asarray(L0_tok_W1),
        "b1": np.asarray(L0_tok_b1).reshape(1, -1),
        "ln_g": np.asarray(L0_tok_ln_g).reshape(1, -1),
        "ln_b_col": col(L0_tok_ln_b),
        "w2": np.asarray(L0_tok_W2),
        "b2x2": col(np.concatenate([L0_tok_b2, L0_tok_b2])),
        "route": np.asarray(L0_ffn_route_id).reshape(1, -1),
        "wi_t": np.asarray(L0_ffn_Wi).T,
        "bi": col(L0_ffn_bi),
        "experts": np.concatenate([wr, br], axis=2),
        "shared": np.concatenate([ws, bs], axis=1),
        "wo_t": np.asarray(L0_ffn_Wo).T,
        "box2": col(np.concatenate([L0_ffn_bo, L0_ffn_bo])),
        "row_mask": row_mask.T.reshape(1, 2 * PARTS, ROWS),
    }
    nc = bacc.Bacc("TRN2", target_bir_lowering=False, num_devices=1)
    given, args = {}, []
    for name, a in arrays.items():
        a = np.ascontiguousarray(a)
        given[f"in_{name}"] = a
        args.append(nc.dram_tensor(f"in_{name}", a.shape, mybir.dt.from_np(a.dtype), kind="ExternalInput").ap())
    args.append(nc.dram_tensor("out_h", (B, T, D), F32, kind="ExternalOutput").ap())
    tower(nc, *args)
    r = run_bass_kernel_spmd(nc, [given], core_ids=[0])
    return r.results[0]["out_h"]
```
